# Optimizing a Trainium2 kernel written in Bass

```python
import numpy as np
import jax
import jax.numpy as jnp

def _softmax(x, axis=-1):
    return jax.nn.softmax(x, axis=axis)

def _gelu(x):
    return jax.nn.gelu(x, approximate=True)

def _silu(x):
    return jax.nn.silu(x)

def _sigmoid(x):
    return jax.nn.sigmoid(x)

def _layernorm(x, axis=-1, eps=1e-05):
    m = jnp.mean(x, axis=axis, keepdims=True)
    v = jnp.var(x, axis=axis, keepdims=True)
    return (x - m) / jnp.sqrt(v + eps)

def _scatter_add(tgt, idx, src, axis=0):
    return tgt.at[idx].add(src)

def _segment_sum(src, seg, n):
    return jax.ops.segment_sum(src, seg, n)
kernel_name = 'mk_lm_tower_d1_tok_ids256_r4_9eec68'

def setup_inputs(seed: int=0):
    np.random.seed(seed)
    _w = jnp.asarray

    def _rec_inputs():
        import jax
        import jax.numpy as jnp
        _rk = jax.random.key(seed)
        x = jax.random.randint(jax.random.fold_in(_rk, 1), (32, 512), 0, 262137, jnp.int32)
        return x
    x = _rec_inputs()

    def _L0_tok_setup():
        import jax, jax.numpy as jnp
        import numpy as np
        NUM_EMB1 = 128
        NUM_EMB2 = 128
        EMB_DIM = 64
        BATCH, SEQ = (16, 1024)
        key = jax.random.key(seed)
        k1, k2, k3, k4, k5 = jax.random.split(key, 5)
        x = jax.random.randint(k1, (BATCH, SEQ), 0, NUM_EMB1 * NUM_EMB2, dtype=jnp.int64 if jax.config.jax_enable_x64 else jnp.int32)
        emb1 = jax.random.normal(k2, (NUM_EMB1, EMB_DIM), dtype=jnp.float32)
        emb2 = jax.random.normal(k3, (NUM_EMB2, EMB_DIM), dtype=jnp.float32)
        lim = 1.0 / np.sqrt(2 * EMB_DIM)
        W = jax.random.uniform(k4, (EMB_DIM, 2 * EMB_DIM), minval=-lim, maxval=lim, dtype=jnp.float32)
        b = jax.random.uniform(k5, (EMB_DIM,), minval=-lim, maxval=lim, dtype=jnp.float32)
        return {'x': x, 'emb1': emb1, 'emb2': emb2, 'W': W, 'b': b}
    _L0_tok_all = _L0_tok_setup()
    _L0_tok_in = {k: v for k, v in _L0_tok_all.items() if k in ('emb1', 'emb2', 'W', 'b')}
    del _L0_tok_all

    def _L0_attn_setup():
        import jax, jax.numpy as jnp
        import numpy as np
        import math
        NUM_HEADS = 8
        HEAD_SIZE = 32

        def get_alibi_slopes(n_heads):

            def pow2_slopes(n):
                start = 2.0 ** (-2.0 ** (-(math.log2(n) - 3)))
                ratio = start
                return [start * ratio ** i for i in range(n)]
            if math.log2(n_heads).is_integer():
                return np.array(pow2_slopes(n_heads), dtype=np.float32)
            cp2 = 2 ** math.floor(math.log2(n_heads))
            extra = pow2_slopes(2 * cp2)[0::2][:n_heads - cp2]
            return np.array(pow2_slopes(cp2) + extra, dtype=np.float32)
        ALIBI_SLOPES = jnp.asarray(get_alibi_slopes(NUM_HEADS))
        key = jax.random.key(seed)
        ks = jax.random.split(key, 6)
        B, T, C = (32, 128, 64)
        s = 1.0 / math.sqrt(C)
        return {'x': jax.random.normal(ks[0], (B, T, C), dtype=jnp.float32), 'Wq': jax.random.normal(ks[1], (C, NUM_HEADS * HEAD_SIZE), dtype=jnp.float32) * s, 'Wk': jax.random.normal(ks[2], (C, NUM_HEADS * HEAD_SIZE), dtype=jnp.float32) * s, 'Wv': jax.random.normal(ks[3], (C, NUM_HEADS * HEAD_SIZE), dtype=jnp.float32) * s, 'Wo': jax.random.normal(ks[4], (NUM_HEADS * HEAD_SIZE, C), dtype=jnp.float32) * s, 'bo': jax.random.normal(ks[5], (C,), dtype=jnp.float32) * 0.01}
    _L0_attn_all = _L0_attn_setup()
    _L0_attn_in = {k: v for k, v in _L0_attn_all.items() if k in ('Wq', 'Wk', 'Wv', 'Wo', 'bo')}
    del _L0_attn_all

    def _L0_ffn_setup():
        import jax, jax.numpy as jnp
        import numpy as np
        IN_CH = 64
        OUT_CH = 64
        key = jax.random.key(seed)
        kx, kw, kb = jax.random.split(key, 3)
        x = jax.random.normal(kx, (8, 1024, IN_CH), dtype=jnp.float32)
        bound = 1.0 / np.sqrt(IN_CH)
        weight = jax.random.uniform(kw, (OUT_CH, IN_CH), dtype=jnp.float32, minval=-bound, maxval=bound)
        bias = jax.random.uniform(kb, (OUT_CH,), dtype=jnp.float32, minval=-bound, maxval=bound)
        return {'x': x, 'weight': weight, 'bias': bias}
    _L0_ffn_all = _L0_ffn_setup()
    _L0_ffn_in = {k: v for k, v in _L0_ffn_all.items() if k in ('weight', 'bias')}
    del _L0_ffn_all
    return {'x': x, 'L0_tok_emb1': _L0_tok_in['emb1'], 'L0_tok_emb2': _L0_tok_in['emb2'], 'L0_tok_W': _L0_tok_in['W'], 'L0_tok_b': _L0_tok_in['b'], 'L0_attn_Wq': _L0_attn_in['Wq'], 'L0_attn_Wk': _L0_attn_in['Wk'], 'L0_attn_Wv': _L0_attn_in['Wv'], 'L0_attn_Wo': _L0_attn_in['Wo'], 'L0_attn_bo': _L0_attn_in['bo'], 'L0_ffn_weight': _L0_ffn_in['weight'], 'L0_ffn_bias': _L0_ffn_in['bias']}

def reference(x, L0_tok_emb1, L0_tok_emb2, L0_tok_W, L0_tok_b, L0_attn_Wq, L0_attn_Wk, L0_attn_Wv, L0_attn_Wo, L0_attn_bo, L0_ffn_weight, L0_ffn_bias):
    import jax
    import jax.numpy as jnp

    def _L0_tok_ref(x, emb1, emb2, W, b):
        import jax, jax.numpy as jnp
        import numpy as np
        NUM_EMB1 = 128
        NUM_EMB2 = 128
        EMB_DIM = 64
        BATCH, SEQ = (16, 1024)
        dim2 = NUM_EMB2
        x1 = emb1[x // dim2]
        x2 = emb2[x % dim2]
        h = jnp.concatenate([x1, x2], axis=-1)
        y = jnp.tanh(jnp.einsum('bsk,dk->bsd', h, W) + b)
        return y

    def _L0_attn_ref(x, Wq, Wk, Wv, Wo, bo):
        import jax, jax.numpy as jnp
        import numpy as np
        import math
        NUM_HEADS = 8
        HEAD_SIZE = 32

        def get_alibi_slopes(n_heads):

            def pow2_slopes(n):
                start = 2.0 ** (-2.0 ** (-(math.log2(n) - 3)))
                ratio = start
                return [start * ratio ** i for i in range(n)]
            if math.log2(n_heads).is_integer():
                return np.array(pow2_slopes(n_heads), dtype=np.float32)
            cp2 = 2 ** math.floor(math.log2(n_heads))
            extra = pow2_slopes(2 * cp2)[0::2][:n_heads - cp2]
            return np.array(pow2_slopes(cp2) + extra, dtype=np.float32)
        ALIBI_SLOPES = jnp.asarray(get_alibi_slopes(NUM_HEADS))
        B, T, C = x.shape
        H, D = (NUM_HEADS, HEAD_SIZE)
        q = (x @ Wq).reshape(B, T, H, D).transpose(0, 2, 1, 3)
        k = (x @ Wk).reshape(B, T, H, D).transpose(0, 2, 1, 3)
        v = (x @ Wv).reshape(B, T, H, D).transpose(0, 2, 1, 3)
        scale = 1.0 / math.sqrt(D)
        wei = jnp.einsum('bhtd,bhsd->bhts', q, k) * scale
        pos = jnp.arange(T)
        rel = (pos[None, :] - pos[:, None]).astype(jnp.float32)
        bias = ALIBI_SLOPES[:, None, None] * rel[None, :, :]
        wei = wei + bias[None]
        causal = pos[None, :] <= pos[:, None]
        wei = jnp.where(causal[None, None], wei, -jnp.inf)
        wei = jax.nn.softmax(wei, axis=-1)
        out = jnp.einsum('bhts,bhsd->bhtd', wei, v)
        out = out.transpose(0, 2, 1, 3).reshape(B, T, H * D)
        return out @ Wo + bo

    def _L0_ffn_ref(x, weight, bias):
        import jax, jax.numpy as jnp
        import numpy as np
        IN_CH = 64
        OUT_CH = 64
        return jnp.einsum('bsi,oi->bso', x, weight) + bias
    h = _L0_tok_ref(x, L0_tok_emb1, L0_tok_emb2, L0_tok_W, L0_tok_b)
    h = h + _L0_attn_ref(_layernorm(h, axis=-1), L0_attn_Wq, L0_attn_Wk, L0_attn_Wv, L0_attn_Wo, L0_attn_bo)
    h = h + _L0_ffn_ref(_layernorm(h, axis=-1), L0_ffn_weight, L0_ffn_bias)
    return h

_drawn_inputs = setup_inputs


def setup_inputs(seed=0):
    import zlib

    import numpy as np

    out = dict(_drawn_inputs(seed))
    spreads = {}
    factors = {'L0_attn_bo': 7.562}
    for name, (base, spread) in spreads.items():
        noise = np.random.default_rng([zlib.crc32(name.encode()), seed]).standard_normal(out[name].shape)
        drawn = base * np.exp(spread * noise) if base else spread * noise
        out[name] = jnp.asarray(drawn.astype(out[name].dtype))
    for name, factor in factors.items():
        out[name] = (out[name] * factor).astype(out[name].dtype)
    return out
```

```python
from contextlib import ExitStack

import concourse.bass as bass
from concourse import mybir

ALU = mybir.AluOpType
ACT = mybir.ActivationFunctionType
AX_X = mybir.AxisListType.X
F32 = mybir.dt.float32
F32R = mybir.dt.float32r
BF16 = mybir.dt.bfloat16
I32 = mybir.dt.int32

P = 128
BATCH, SEQ, C = 32, 512, 64
CODES = 128
H, D = 8, 32
HG = 4
GROUPS = H // HG
T = SEQ // P
SCALE = float(D) ** -0.5
EPS = 1e-5
SLOPES = [2.0 ** -(h + 1) for h in range(H)]
MASKED = -3.0e38
SHIFT = CODES.bit_length() - 1
QK_ROWS = 3 * D
ALIBI_ROWS = QK_ROWS + 2
ALL_ROWS = ALIBI_ROWS + 2
PAIR_BANKS = 5
UNIT_BANKS = 2 * PAIR_BANKS
STEPS = GROUPS * UNIT_BANKS
LAG = 15
STACK_DMAS = HG * 3


def bank_blocks(k):
    if k == 4:
        return [(0, 2, 0), (1, 2, 2 * P)]
    if k % 2 == 0:
        return [(k // 2, 4, 0)]
    return [(k // 2, 3, 0), (k // 2, 1, 3 * P)]


def block_place(h, extent):
    for k in range(PAIR_BANKS):
        for hh, e, col in bank_blocks(k):
            if hh == h and e == extent:
                return k, col


def build(nc, x, emb1, emb2, tok_w, tok_b, wq, wk, wv, wo, bo, ffn_w, ffn_b, out):
    codes_dram = nc.dram_tensor("codes_scratch", (2, BATCH * SEQ), BF16, kind="Internal").ap()
    out_rows = out.rearrange("b (t p) c -> b p t c", p=P)

    with ExitStack() as ctx:
        def sb(name, shape, dt=F32):
            return ctx.enter_context(nc.sbuf_tensor(name, shape, dt))

        def bank(name, dt=F32):
            return ctx.enter_context(nc.psum_tensor(name, [P, 512], dt))

        def sem(name):
            return ctx.enter_context(nc.semaphore(name))

        h_all = sb("h_all", [P, BATCH, T, C])
        stack = [sb(f"stack{i}", [P, 2, H, SEQ], F32R) for i in range(2)]
        probs = sb("probs", [P, GROUPS, 2, PAIR_BANKS, 512])
        values = [sb(f"values{i}", [P, T, H, D]) for i in range(2)]
        nat = [sb(f"nat{g}", [P, 4, SEQ], F32R) for g in range(GROUPS)]
        xs = [sb(f"xs{i}", [P, SEQ], F32R) for i in range(2)]
        x2 = sb("x2", [P, T, 2, C])
        centred = sb("centred", [P, T, C])
        centred2 = sb("centred2", [P, T, C])
        ffn_in = sb("ffn_in", [P, T, 2, C])
        ffn_in_t = sb("ffn_in_t", [P, SEQ])
        h_bo = sb("h_bo", [P, T, C])
        mixed = [sb(f"mixed{g}", [P, SEQ]) for g in range(GROUPS)]
        log_sum = sb("log_sum", [P, SEQ])
        inv_sum = sb("inv_sum", [P, SEQ])
        out_sb = sb("out_sb", [P, T, C])
        w_hi = sb("w_hi", [P, 3 * H * D], F32R)
        w_lo = sb("w_lo", [P, 3 * H * D], F32R)
        wo_sb = sb("wo_sb", [P, GROUPS, C])
        ffn_rhs = sb("ffn_rhs", [P, C])
        bo_bc = sb("bo_bc", [P, C])
        ffn_b_bc = sb("ffn_b_bc", [P, C])
        tok_b_bc = sb("tok_b_bc", [P, C])
        ident = sb("ident", [P, P])
        ident_bf = sb("ident_bf", [P, P], BF16)
        causal = sb("causal", [P, P], BF16)
        ones = sb("ones", [P, D])
        eps = sb("eps", [P, 1])
        code_id = sb("code_id", [P, 1])
        neg_max = [sb(f"neg_max{g}", [P, HG * T]) for g in range(GROUPS)]
        nm_parts = [sb(f"nm_parts{g}", [P, 2, HG * T], F32R) for g in range(GROUPS)]
        nm_rows = [sb(f"nm_rows{g}", [2 * HG * T, P], F32R) for g in range(GROUPS)]
        bn1 = sb("bn1", [P, T, 6])
        bn2 = sb("bn2", [P, T, 6])
        mv1 = sb("mv1", [P, T, 2])
        mv2 = sb("mv2", [P, T, 2])
        logv = sb("logv", [P, 2, T])
        rstd1 = sb("rstd1", [P, T])
        rstd2 = sb("rstd2", [P, T])
        tabs = sb("tabs", [P, 2, 3, C], BF16)
        tab_rest = sb("tab_rest", [P, 2, 2, C])
        stage = probs[:, 0, 0, 0:2, :].rearrange("p a c -> p (a c)")[:, 0:3 * H * D]
        pos = probs[:, 0, 0, 2, :]
        emb_in = probs[:, 0, 0, 3, 0:2 * C]
        tokw_in = probs[:, 0, 0, 3, P:2 * P]
        embT = probs[:, 0, 0, 3, 2 * P:3 * P]
        tokwT = probs[:, 0, 0, 3, 3 * P:3 * P + C]
        ffnw_in = probs[:, 0, 0, 4, 0:C]
        coef = probs[:, 0, 0, 4, C:C + 4 * H].rearrange("p (a h) -> p a h", a=4)
        tok = probs[:, 0, 1, 0, 0:P].bitcast(I32)
        tok_code = probs[:, 0, 1, 1, 0:2 * P].bitcast(I32).rearrange("p (e n) -> p e n", e=2)
        tok_f = probs[:, 0, 1, 2, 0:P]
        tok_bf = probs[:, 0, 1, 3, 0:P].bitcast(BF16).rearrange("p (e n) -> p e n", e=2)
        iota_i = probs[:, 0, 1, 4, :].bitcast(I32)
        code_bc = [probs[:, 1, 0, i, :].bitcast(BF16).rearrange("p (e n) -> p e n", e=2) for i in range(2)]
        onehot = [probs[:, 1, 1, i, :].bitcast(BF16).rearrange("p (e n) -> p e n", e=2) for i in range(2)]

        m_bank = [bank(f"m_bank{i}") for i in range(2)]
        s_bank = [bank(f"s_bank{i}") for i in range(2)]
        o_bank = bank("o_bank")
        l_bank = bank("l_bank")
        a_bank = bank("a_bank")
        b_bank = bank("b_bank")

        loaded = sem("loaded")
        tok_loaded = sem("tok_loaded")
        const = sem("const")
        vconst = sem("vconst")
        pconst = sem("pconst")
        codes_stored = sem("codes_stored")
        code_loaded = [sem(f"code_loaded{i}") for i in range(2)]
        onehot_done = sem("onehot_done")
        emb_ready = sem("emb_ready")
        h_done = sem("h_done")
        x_ready = sem("x_ready")
        xt_ready = sem("xt_ready")
        xh_done = sem("xh_done")
        x_split = sem("x_split")
        qk_ready = sem("qk_ready")
        qk_hi = sem("qk_hi")
        qk_split = sem("qk_split")
        stacked = [sem(f"stacked{g}") for g in range(GROUPS)]
        v_ready = sem("v_ready")
        v_done = sem("v_done")
        m_ready = sem("m_ready")
        m_used = sem("m_used")
        nm_high = sem("nm_high")
        nm_split = sem("nm_split")
        nmt_ready = sem("nmt_ready")
        nm_row = sem("nm_row")
        nm_loaded = [sem(f"nm_loaded{g}") for g in range(GROUPS)]
        s_ready = sem("s_ready")
        exp_done = sem("exp_done")
        masked = sem("masked")
        mix_done = sem("mix_done")
        sum_log = sem("sum_log")
        inv_ready = sem("inv_ready")
        mixed_done = sem("mixed_done")
        h_bo_ready = sem("h_bo_ready")
        y_ready = sem("y_ready")
        res_done = sem("res_done")
        bn2_done = sem("bn2_done")
        mv2_done = sem("mv2_done")
        log2_done = sem("log2_done")
        rstd2_done = sem("rstd2_done")
        cen2_done = sem("cen2_done")
        x2_ready = sem("x2_ready")
        ft_ready = sem("ft_ready")
        ft_done = sem("ft_done")
        fo_ready = sem("fo_ready")
        out_ready = sem("out_ready")
        out_stored = sem("out_stored")
        bn1_done = sem("bn1_done")
        mv1_done = sem("mv1_done")
        log1_done = sem("log1_done")
        rstd1_done = sem("rstd1_done")
        cen1_done = sem("cen1_done")

        held = {e: sem(f"held_{n}") for n, e in (("sp", mybir.EngineType.SP), ("pool", mybir.EngineType.Pool),
                                                 ("dve", mybir.EngineType.DVE))}

        class Row:

            def __init__(self, b, parity, looped):
                self.b, self.parity, self.looped = b, parity, looped

            def has(self, d):
                return self.looped or 0 <= self.b + d < BATCH

            def par(self, d):
                return (self.parity + d) % 2

        def await_count(eng, semaphore, value):
            if not isinstance(value, int) or value > 0:
                eng.wait_ge(semaphore, value)

        def hold(eng):
            eng.sem_inc(held[eng.engine], 1)

        def over_rows(eng, iteration):
            for b in range(-2, 4):
                iteration(Row(b, b % 2, False))
            with eng.Fori(2, BATCH // 2 - 1) as pair:
                iteration(Row(2 * pair, 0, True))
                iteration(Row(2 * pair + 1, 1, True))
            for b in range(BATCH - 2, BATCH + 2):
                iteration(Row(b, b % 2, False))

        def weight_bank(row, r):
            return (-1, r + STEPS - LAG) if r < LAG else (0, r - LAG)

        A_QK = {2: 0, 4: 1, 7: 2, 9: 3}
        A_V = {14: 0, 16: 1}
        MIX = {7: (-1, 0, 0), 9: (-1, 0, 1), 11: (-1, 0, 2), 13: (-1, 0, 3),
               17: (-1, 1, 0), 19: (-1, 1, 1), 1: (-2, 1, 2), 3: (-2, 1, 3)}
        MAX_ROWS = {1: (-1, 1), 11: (0, 0)}
        NORM = {4: (-2, 1), 14: (-1, 0)}

        B_JOBS = {"max1": (-1, nm_row, 2, 2), "y": (-2, res_done, 1, 1), "max0": (0, nm_row, 2, 1),
                  "ft": (-2, ft_done, 1, 1), "fo": (-2, out_ready, 1, 1)}

        def await_b_bank(eng, row, job):
            names = list(B_JOBS)
            at = names.index(job)
            for back in range(1, 2 * len(names)):
                k = at - back
                name, shift = names[k % len(names)], k // len(names)
                d, semaphore, per_row, n = B_JOBS[name]
                if row.has(d + shift):
                    await_count(eng, semaphore, per_row * (row.b + d + shift) + n)
                    return

        block = ctx.enter_context(nc.Block())

        @block.sync
        def _(sp):
            sp.dma_start(tok, x.rearrange("b (q n) -> (b q) n", n=P)).then_inc(tok_loaded, 16)
            with nc.allow_non_contiguous_dma("weights and broadcasts, once"):
                for half in (0, C):
                    for n, w in enumerate((wq, wk, wv)):
                        sp.dma_start(stage[half:half + C, n * H * D:(n + 1) * H * D], w).then_inc(loaded, 16)
                sp.dma_start(wo_sb[:], wo.rearrange("(g p) c -> p g c", p=P)).then_inc(loaded, 16)
                sp.dma_start(emb_in[:, 0:C], emb1).then_inc(loaded, 16)
                sp.dma_start(emb_in[:, C:2 * C], emb2).then_inc(loaded, 16)
                sp.dma_start(tokw_in[0:C, :], tok_w).then_inc(loaded, 16)
                sp.dma_start(ffnw_in[0:C, :], ffn_w).then_inc(loaded, 16)
                for dst, src in ((bo_bc, bo), (ffn_b_bc, ffn_b), (tok_b_bc, tok_b)):
                    sp.dma_start(dst[:], src.partition_broadcast(P)).then_inc(loaded, 16)

                sp.wait_ge(vconst, 6)
                sp.dma_start(codes_dram.rearrange("e (p n) -> p e n", n=P), tok_bf).then_inc(codes_stored, 16)
                sp.wait_ge(codes_stored, 16)

                def load_codes(b, par):
                    sp.dma_start(code_bc[par],
                                 codes_dram[:, bass.ds(b * SEQ, SEQ)].partition_broadcast(P)
                                 ).then_inc(code_loaded[par], 16)

                for par in range(2):
                    load_codes(par, par)
                with sp.Fori(1, BATCH // 2) as pair:
                    for par in range(2):
                        sp.wait_ge(onehot_done, 2 * pair + par - 1)
                        load_codes(2 * pair + par, par)

            def load_max_rows(row, d, g):
                if row.has(d):
                    n = row.b + d
                    sp.wait_ge(nm_row, 2 * n + g + 1)
                    sp.dma_start(stack[row.par(d)][ALIBI_ROWS:ALL_ROWS, 0, g * HG:(g + 1) * HG, :].bitcast(F32),
                                 nm_rows[g][:].bitcast(F32)).then_inc(nm_loaded[g], 16)

            def load_stacks(row, g):
                if row.has(1):
                    n = row.b + 1
                    await_count(sp, s_ready, STEPS * (n - 2) + UNIT_BANKS * (g + 1))
                    hold(sp)
                    sp.wait_ge(qk_split, 4 * n + 2 * g + 2)
                    for j in range(HG):
                        for s, parts in enumerate((slice(0, 3, 2), slice(1, 3), slice(1, 4, 2))):
                            sp.dma_start(stack[row.par(1)][s * D:(s + 1) * D, :, g * HG + j, :].bitcast(F32),
                                         nat[g][j * D:(j + 1) * D, parts, :].bitcast(F32)).then_inc(stacked[g], 16)

            def iteration(row):
                load_max_rows(row, -1, 1)
                load_stacks(row, 0)
                load_max_rows(row, 0, 0)
                load_stacks(row, 1)
                if row.has(-2):
                    n = row.b - 2
                    sp.wait_ge(out_ready, n + 1)
                    sp.dma_start(out_rows[n] if isinstance(n, int) else
                                 out_rows[bass.ds(n, 1)].rearrange("o p t c -> (o p) t c"),
                                 out_sb[:]).then_inc(out_stored, 16)

            over_rows(sp, iteration)
            sp.wait_ge(out_stored, 16 * BATCH)

        @block.gpsimd
        def _(pool):
            count = [0]

            def step(ins):
                count[0] += 1
                ins.then_inc(const, 1)
                pool.wait_ge(const, count[0])

            step(pool.memset(ident[:], 0.0))
            step(pool.affine_select(out=ident[:], in_=ident[:], compare_op=ALU.not_equal, fill=1.0, base=0,
                                    pattern=[[-1, P]], channel_multiplier=1))
            step(pool.tensor_copy(ident_bf[:], ident[:]))
            step(pool.memset(causal[:], 0.0))
            step(pool.affine_select(out=causal[:], in_=causal[:], compare_op=ALU.is_ge, fill=MASKED, base=0,
                                    pattern=[[-1, P]], channel_multiplier=1))
            step(pool.memset(ones[:], 1.0))
            step(pool.memset(eps[:], EPS))
            step(pool.iota(code_id[:], pattern=[[0, 1]], base=0, channel_multiplier=1,
                           allow_small_or_imprecise_dtypes=True))
            step(pool.iota(iota_i, pattern=[[1, SEQ]], base=0, channel_multiplier=0))
            step(pool.tensor_copy(pos, iota_i))
            for n, (value, row_value, at) in enumerate(
                    [(0.0, None, 1), (0.0, 1.0, 0), (0.0, None, 0), (1.0, 0.0, 0)]):
                step(pool.memset(coef[:, n, :], value))
                if row_value is None:
                    for h in range(H):
                        step(pool.affine_select(out=coef[:, n, h:h + 1], in_=coef[:, n, h:h + 1],
                                                compare_op=ALU.not_equal,
                                                fill=-SLOPES[h] if at else SLOPES[h], base=-(QK_ROWS + at),
                                                pattern=[[0, 1]], channel_multiplier=1))
                else:
                    step(pool.affine_select(out=coef[:, n, :], in_=coef[:, n, :], compare_op=ALU.not_equal,
                                            fill=row_value, base=-(QK_ROWS + at), pattern=[[0, H]],
                                            channel_multiplier=1))
            assert count[0] == CONST_STEPS

            def diagonals(row, d, pair):
                if row.has(d):
                    n = row.b + d
                    g, half = divmod(pair, 2)
                    pool.wait_ge(exp_done, STEPS * n + PAIR_BANKS * (pair + 1))
                    hold(pool)
                    banks = probs[:, g, half, :, :]
                    for part, width in ((banks[:, :, 0:P], 5), (banks[:, 1:4:2, 3 * P:4 * P], 2),
                                        (banks[:, 4:5, 2 * P:3 * P], 1)):
                        ins = pool.affine_select(out=part, in_=part, compare_op=ALU.is_ge, fill=0.0, base=0,
                                                 pattern=[[0, width], [1, P]], channel_multiplier=-1)
                    ins.then_inc(masked, 1)

            def iteration(row):
                if row.has(-2):
                    n = row.b - 2
                    await_count(pool, res_done, n)
                    pool.wait_ge(h_done, BATCH)
                    pool.tensor_tensor(h_bo[:], h_all[:, n, :, :] if isinstance(n, int) else
                                       h_all[:, bass.ds(n, 1), :, :].rearrange("p o t c -> p (o t) c"),
                                       bo_bc[:, :].unsqueeze(1).broadcast_to([P, T, C]),
                                       ALU.add).then_inc(h_bo_ready, 1)
                diagonals(row, -1, 1)
                diagonals(row, -1, 2)
                if row.has(-2):
                    n = row.b - 2
                    pool.wait_ge(mv2_done, n + 1)
                    pool.tensor_tensor(centred2[:], ffn_in[:, :, 1, :],
                                       mv2[:, :, 0:1].broadcast_to([P, T, C]), ALU.subtract).then_inc(cen2_done, 1)
                    pool.wait_ge(cen2_done, n + 1)
                    pool.wait_ge(rstd2_done, n + 1)
                    await_count(pool, ft_ready, n)
                    pool.tensor_tensor(ffn_in[:, :, 0, :], centred2[:],
                                       rstd2[:, :].unsqueeze(2).broadcast_to([P, T, C]),
                                       ALU.mult).then_inc(x2_ready, 1)
                diagonals(row, -1, 3)
                if row.has(2):
                    n = row.b + 2
                    pool.wait_ge(mv1_done, n + 1)
                    pool.wait_ge(h_done, BATCH)
                    pool.tensor_tensor(centred[:], h_all[:, n, :, :] if isinstance(n, int) else
                                       h_all[:, bass.ds(n, 1), :, :].rearrange("p o t c -> p (o t) c"),
                                       mv1[:, :, 0:1].broadcast_to([P, T, C]), ALU.subtract).then_inc(cen1_done, 1)
                    pool.wait_ge(cen1_done, n + 1)
                    pool.wait_ge(rstd1_done, n + 1)
                    await_count(pool, xt_ready, n)
                    for copy in range(2):
                        ins = pool.tensor_tensor(x2[:, :, copy, :], centred[:],
                                                 rstd1[:, :].unsqueeze(2).broadcast_to([P, T, C]), ALU.mult)
                    ins.then_inc(x_ready, 1)
                diagonals(row, 0, 0)

            over_rows(pool, iteration)

        @block.scalar
        def _(act):
            def tanh_rows(b, par):
                act.wait_ge(emb_ready, b + 1)
                act.wait_ge(const, CONST_STEPS)
                dst = (h_all[:, b, :, :].rearrange("p t c -> p (t c)") if isinstance(b, int) else
                       h_all[:, bass.ds(b, 1), :, :].rearrange("p o t c -> p (o t c)"))
                act.activation(dst, m_bank[par][:, 0:T * C], ACT.Tanh).then_inc(h_done, 1)

            for par in range(2):
                tanh_rows(par, par)
            with act.Fori(1, BATCH // 2) as pair:
                for par in range(2):
                    tanh_rows(2 * pair + par, par)
            act.preload_act_table_set("natural_log_exp_and_others")

            def exp_bank(row, r):
                d, idx = weight_bank(row, r)
                if not row.has(d):
                    return
                n, g = row.b + d, idx // UNIT_BANKS
                half, k = divmod(idx % UNIT_BANKS, PAIR_BANKS)
                if idx % UNIT_BANKS == 0:
                    await_count(act, mix_done, 8 * (n - 1) + 4 * g + 4)
                act.wait_ge(s_ready, STEPS * n + idx + 1)
                act.activation(probs[:, g, half, k, :], s_bank[idx % 2][:], ACT.Exp).then_inc(exp_done, 1)

            def x_high(row):
                if row.has(1):
                    n = row.b + 1
                    act.wait_ge(xt_ready, n + 1)
                    await_count(act, v_ready, 2 * (n - 2) + 2)
                    act.copy(xs[row.par(1)][:], a_bank[:]).then_inc(xh_done, 1)

            def qk_high(row, c):
                if row.has(1):
                    n, g = row.b + 1, c // 2
                    await_count(act, stacked[g], 16 * STACK_DMAS * n)
                    act.wait_ge(qk_ready, 4 * n + c + 1)
                    if c % 2 == 0:
                        ins = act.mul(nat[g][:, 1, :], a_bank[:], SCALE)
                    else:
                        ins = act.copy(nat[g][:, 2, :], a_bank[:])
                    ins.then_inc(qk_hi, 1)

            def copy_values(row, c):
                if row.has(0):
                    await_count(act, mix_done, 8 * (row.b - 2) + 8)
                    act.wait_ge(v_ready, 2 * row.b + c + 1)
                    act.copy(values[row.par(0)][:, 2 * c:2 * c + 2, :, :],
                             a_bank[:].rearrange("p (t h d) -> p t h d", t=2, h=H)).then_inc(v_done, 1)

            def copy_max_rows(row, d, g):
                if row.has(d):
                    n = row.b + d
                    await_count(act, nm_loaded[g], 16 * n)
                    act.wait_ge(nmt_ready, 2 * n + g + 1)
                    act.copy(nm_rows[g][:], b_bank[0:2 * HG * T, 0:P]).then_inc(nm_row, 1)

            def invert_sums(row, d, g):
                if row.has(d):
                    n = row.b + d
                    act.wait_ge(mix_done, 8 * n + 4 * g + 4)
                    act.activation(log_sum[:], l_bank[:], ACT.Ln).then_inc(sum_log, 1)
                    await_count(act, mixed_done, 2 * n + g)
                    act.wait_ge(sum_log, 2 * n + g + 1)
                    act.activation(inv_sum[:], log_sum[:], ACT.Exp, scale=-1.0).then_inc(inv_ready, 1)

            def rsqrt(n, which, mv, mv_done, log_done, rstd, rstd_used, rstd_done):
                act.wait_ge(mv_done, n + 1)
                act.activation(logv[:, which, :].unsqueeze(2), mv[:, :, 1:2], ACT.Ln,
                               bias=eps[:, 0:1]).then_inc(log_done, 1)
                await_count(act, rstd_used, n)
                act.wait_ge(log_done, n + 1)
                act.activation(rstd[:], logv[:, which, :], ACT.Exp, scale=-0.5).then_inc(rstd_done, 1)

            def iteration(row):
                for r in range(STEPS):
                    exp_bank(row, r)
                    if r == 1:
                        x_high(row)
                    if r - 1 in A_QK:
                        qk_high(row, A_QK[r - 1])
                    if r - 1 in A_V:
                        copy_values(row, A_V[r - 1])
                    if r - 1 in MAX_ROWS:
                        copy_max_rows(row, *MAX_ROWS[r - 1])
                    if r in NORM:
                        invert_sums(row, *NORM[r])
                    if r == 8 and row.has(-2):
                        rsqrt(row.b - 2, 1, mv2, mv2_done, log2_done, rstd2, x2_ready, rstd2_done)
                    if r == 12 and row.has(2):
                        rsqrt(row.b + 2, 0, mv1, mv1_done, log1_done, rstd1, x_ready, rstd1_done)
                    if r == 14 and row.has(-2):
                        n = row.b - 2
                        await_count(act, fo_ready, n)
                        act.wait_ge(ft_ready, n + 1)
                        act.copy(ffn_in_t[:], b_bank[:]).then_inc(ft_done, 1)

            over_rows(act, iteration)

        @block.vector
        def _(dve):
            count = [0]

            def step(ins):
                count[0] += 1
                ins.then_inc(vconst, 1)
                dve.wait_ge(vconst, count[0])

            dve.wait_ge(tok_loaded, 16)
            step(dve.tensor_scalar(tok_code[:, 0, :], tok, SHIFT, None, ALU.arith_shift_right))
            step(dve.tensor_scalar(tok_code[:, 1, :], tok, CODES - 1, None, ALU.bitwise_and))
            step(dve.tensor_copy(tok_f, tok_code[:, 0, :]))
            step(dve.tensor_scalar(tok_f, tok_f, 0.0, float(CODES - 1), ALU.max, ALU.min))
            step(dve.tensor_copy(tok_bf[:, 0, :], tok_f))
            step(dve.tensor_copy(tok_bf[:, 1, :], tok_code[:, 1, :]))

            dve.wait_ge(loaded, 16 * LOADS)
            dve.wait_ge(pconst, 2)
            dve.tensor_copy(embT, a_bank[:, 0:P]).then_inc(vconst, 1)
            dve.tensor_copy(tokwT, a_bank[:, P:P + C]).then_inc(vconst, 1)
            dve.tensor_copy(ffn_rhs[0:C, :], a_bank[0:C, 2 * P:2 * P + C]).then_inc(vconst, 1)
            dve.tensor_copy(ffn_rhs[C:P, :], ident[C:P, C:P]).then_inc(vconst, 1)
            count[0] += 4
            dve.wait_ge(pconst, 4)
            step(dve.tensor_tensor(tab_rest[:, 0, 0, :], b_bank[:, 0:C], tok_b_bc[:], ALU.add))
            step(dve.tensor_copy(tab_rest[:, 1, 0, :], o_bank[:, 0:C]))
            step(dve.tensor_copy(tabs[:, :, 0, :], tab_rest[:, :, 0, :]))
            step(dve.tensor_tensor(tab_rest[:, :, 1, :], tab_rest[:, :, 0, :], tabs[:, :, 0, :], ALU.subtract))
            step(dve.tensor_copy(tabs[:, :, 1, :], tab_rest[:, :, 1, :]))
            step(dve.tensor_tensor(tab_rest[:, :, 0, :], tab_rest[:, :, 1, :], tabs[:, :, 1, :], ALU.subtract))
            step(dve.tensor_copy(tabs[:, :, 2, :], tab_rest[:, :, 0, :]))
            assert count[0] == TABLE_STEPS

            step(dve.tensor_copy(w_hi[:], stage))
            step(dve.tensor_tensor(w_lo[:], stage, w_hi[:].bitcast(F32), ALU.subtract))
            dve.wait_ge(const, CONST_STEPS)
            for i in range(2):
                for side in range(2):
                    for h in range(H):
                        ins = dve.tensor_scalar(stack[i][QK_ROWS:ALL_ROWS, side, h, :], pos[QK_ROWS:ALL_ROWS, :],
                                                coef[QK_ROWS:ALL_ROWS, 2 * side, h:h + 1],
                                                coef[QK_ROWS:ALL_ROWS, 2 * side + 1, h:h + 1], ALU.mult, ALU.add)
            step(ins)
            assert count[0] == SETUP_STEPS

            def one_hot(b, par):
                dve.wait_ge(code_loaded[par], 16 * (b // 2 + 1) if isinstance(b, int) else b * 8 - 8 * par + 16)
                if not isinstance(b, int):
                    dve.wait_ge(emb_ready, b - 1)
                dve.tensor_scalar(onehot[par], code_bc[par], code_id[:, 0:1], None,
                                  ALU.is_equal).then_inc(onehot_done, 1)

            for par in range(2):
                one_hot(par, par)
            with dve.Fori(1, BATCH // 2) as pair:
                for par in range(2):
                    one_hot(2 * pair + par, par)

            def maxima(row, r):
                if not row.has(0):
                    return
                g, idx = divmod(r, UNIT_BANKS)
                half, k = divmod(idx, PAIR_BANKS)
                src = m_bank[r % 2]
                view = neg_max[g][:, :].rearrange("p (h t) -> p h t", t=T)
                dve.wait_ge(m_ready, STEPS * row.b + r + 1)
                if k == 4:
                    ins = dve.tensor_reduce(view[:, 2 * half:2 * half + 2, 1:2],
                                            src[:].rearrange("p (h s) -> p h s", h=2), AX_X, ALU.max, negate=True)
                else:
                    for h, extent, col in bank_blocks(k):
                        ins = dve.tensor_reduce(view[:, 2 * half + h, extent - 1:extent],
                                                src[:, col:col + extent * P], AX_X, ALU.max, negate=True)
                ins.then_inc(m_used, 1)

            def split_max(row, d, g):
                if row.has(d):
                    n = row.b + d
                    await_count(dve, nmt_ready, 2 * (n - 1) + g + 1)
                    dve.wait_ge(m_used, STEPS * n + UNIT_BANKS * (g + 1))
                    dve.tensor_copy(nm_parts[g][:, 0, :], neg_max[g][:]).then_inc(nm_high, 1)
                    dve.wait_ge(nm_high, 2 * n + g + 1)
                    dve.tensor_tensor(nm_parts[g][:, 1, :], neg_max[g][:], nm_parts[g][:, 0, :].bitcast(F32),
                                      ALU.subtract).then_inc(nm_split, 1)

            def x_low(row):
                if row.has(1):
                    n = row.b + 1
                    lo = xs[row.par(1)][C:P, :]
                    dve.wait_ge(xh_done, n + 1)
                    dve.tensor_tensor(lo, a_bank[C:P, :], lo.bitcast(F32), ALU.subtract).then_inc(x_split, 1)

            def qk_low(row, c):
                if row.has(1):
                    n, g = row.b + 1, c // 2
                    dve.wait_ge(qk_hi, 4 * n + c + 1)
                    if c % 2 == 0:
                        ins = dve.scalar_tensor_tensor(out=nat[g][:, 0, :], in0=a_bank[:], scalar=SCALE,
                                                       in1=nat[g][:, 1, :].bitcast(F32), op0=ALU.mult,
                                                       op1=ALU.subtract)
                    else:
                        ins = dve.tensor_tensor(nat[g][:, 3, :], a_bank[:], nat[g][:, 2, :].bitcast(F32),
                                                ALU.subtract)
                    ins.then_inc(qk_split, 1)

            def normalise(row, d, g):
                if row.has(d):
                    n = row.b + d
                    await_count(dve, y_ready, n)
                    dve.wait_ge(inv_ready, 2 * n + g + 1)
                    dve.tensor_tensor(mixed[g][:], o_bank[:], inv_sum[:], ALU.mult).then_inc(mixed_done, 1)

            def residual(row):
                if row.has(-2):
                    n = row.b - 2
                    dve.wait_ge(h_bo_ready, n + 1)
                    await_count(dve, ft_ready, n)
                    dve.wait_ge(y_ready, n + 1)
                    dve.tensor_tensor(ffn_in[:, :, 1, :], b_bank[:, 0:T * C].rearrange("p (t c) -> p t c", t=T),
                                      h_bo[:], ALU.add).then_inc(res_done, 1)
                    dve.wait_ge(res_done, n + 1)
                    for t in range(T):
                        ins = dve.bn_stats(bn2[:, t, :], ffn_in[:, t, 1, :])
                    ins.then_inc(bn2_done, 1)
                    dve.wait_ge(bn2_done, n + 1)
                    await_count(dve, rstd2_done, n)
                    await_count(dve, x2_ready, n)
                    hold(dve)
                    for t in range(T):
                        ins = dve.bn_aggr(mv2[:, t, :], bn2[:, t, :])
                    ins.then_inc(mv2_done, 1)

            def statistics(row):
                if row.has(2):
                    n = row.b + 2
                    for t in range(T):
                        src = (h_all[:, n, t, :] if isinstance(n, int) else
                               h_all[:, bass.ds(n, 1), t, :].rearrange("p o c -> p (o c)"))
                        if t == 0:
                            dve.wait_ge(h_done, BATCH)
                        ins = dve.bn_stats(bn1[:, t, :], src)
                    ins.then_inc(bn1_done, 1)
                    dve.wait_ge(bn1_done, n + 1)
                    await_count(dve, rstd1_done, n)
                    await_count(dve, cen1_done, n)
                    hold(dve)
                    for t in range(T):
                        ins = dve.bn_aggr(mv1[:, t, :], bn1[:, t, :])
                    ins.then_inc(mv1_done, 1)

            def add_ffn_bias(row):
                if row.has(-2):
                    n = row.b - 2
                    await_count(dve, out_stored, 16 * n)
                    dve.wait_ge(fo_ready, n + 1)
                    dve.tensor_tensor(out_sb[:], b_bank[:, 0:T * C].rearrange("p (t c) -> p t c", t=T),
                                      ffn_b_bc[:, :].unsqueeze(1).broadcast_to([P, T, C]),
                                      ALU.add).then_inc(out_ready, 1)

            def iteration(row):
                for r in range(STEPS):
                    if r == 0:
                        split_max(row, -1, 1)
                    if r == UNIT_BANKS:
                        split_max(row, 0, 0)
                    maxima(row, r)
                    if r == 1:
                        x_low(row)
                    if r - 1 in A_QK:
                        qk_low(row, A_QK[r - 1])
                    if r - 1 in NORM:
                        normalise(row, *NORM[r - 1])
                    if r == 7:
                        residual(row)
                    if r == 9:
                        statistics(row)
                    if r == 17:
                        add_ffn_bias(row)

            over_rows(dve, iteration)

        @block.tensor
        def _(pe):
            pe.wait_ge(const, CONST_STEPS)
            pe.wait_ge(loaded, 16 * LOADS)
            pe.transpose(a_bank[:, 0:P], emb_in, ident[:])
            pe.transpose(a_bank[:, P:P + C], tokw_in[0:C, :], ident[0:C, 0:C]).then_inc(pconst, 1)
            pe.transpose(a_bank[0:C, 2 * P:2 * P + C], ffnw_in[0:C, :], ident[0:C, 0:C]).then_inc(pconst, 1)
            pe.wait_ge(vconst, 8)
            pe.matmul(b_bank[:, 0:C], embT[0:C, :], tokwT[0:C, :], start=True, stop=True).then_inc(pconst, 1)
            pe.matmul(o_bank[:, 0:C], embT[C:P, :], tokwT[C:P, :], start=True, stop=True).then_inc(pconst, 1)
            pe.wait_ge(vconst, TABLE_STEPS)

            def embed(b, par):
                pe.wait_ge(onehot_done, b + 1)
                if not isinstance(b, int):
                    pe.wait_ge(h_done, b - 1)
                for t in range(T):
                    for e in range(2):
                        for part in range(3):
                            ins = pe.matmul(m_bank[par][:, t * C:(t + 1) * C],
                                            onehot[par][:, e, t * P:(t + 1) * P], tabs[:, e, part, :],
                                            start=(e == 0 and part == 0), stop=(e == 1 and part == 2))
                ins.then_inc(emb_ready, 1)

            for par in range(2):
                embed(par, par)
            with pe.Fori(1, BATCH // 2) as pair:
                for par in range(2):
                    embed(2 * pair + par, par)
            pe.wait_ge(h_done, BATCH)
            pe.wait_ge(vconst, SETUP_STEPS)

            def max_scores(row, r):
                if not row.has(0):
                    return
                g, idx = divmod(r, UNIT_BANKS)
                half, k = divmod(idx, PAIR_BANKS)
                st, dst = stack[row.par(0)], m_bank[r % 2]
                if idx == 0:
                    pe.wait_ge(stacked[g], 16 * STACK_DMAS * (row.b + 1))
                await_count(pe, m_used, STEPS * row.b + r - 1)
                for hh, extent, col in bank_blocks(k):
                    head, diag = g * HG + 2 * half + hh, (extent - 1) * P
                    pe.matmul(dst[:, col:col + extent * P], st[0:ALIBI_ROWS, 0, head, diag:diag + P],
                              st[0:ALIBI_ROWS, 1, head, 0:extent * P], start=True, stop=False)
                    ins = pe.matmul(dst[:, col + diag:col + diag + P], ident_bf[:], causal[:],
                                    start=False, stop=True)
                ins.then_inc(m_ready, 1)

            def weight_scores(row, r):
                d, index = weight_bank(row, r)
                if not row.has(d):
                    return
                n = row.b + d
                g, idx = divmod(index, UNIT_BANKS)
                half, k = divmod(idx, PAIR_BANKS)
                st, dst = stack[row.par(d)], s_bank[index % 2]
                if idx == 0:
                    pe.wait_ge(nm_loaded[g], 16 * (n + 1))
                await_count(pe, exp_done, STEPS * n + index - 1)
                for hh, extent, col in bank_blocks(k):
                    head, first = g * HG + 2 * half + hh, SEQ - extent * P
                    ins = pe.matmul(dst[:, col:col + extent * P], st[0:ALL_ROWS, 1, head, first:first + P],
                                    st[0:ALL_ROWS, 0, head, first:SEQ], start=True, stop=True)
                ins.then_inc(s_ready, 1)

            def mix(row, d, g, i):
                if not row.has(d):
                    return
                n = row.b + d
                if i == 0:
                    pe.wait_ge(masked, 4 * n + 2 * g + 2)
                    pe.wait_ge(v_done, 2 * n + 2)
                    await_count(pe, sum_log, 2 * n + g)
                    await_count(pe, mixed_done, 2 * n + g)
                for dst, weights in ((o_bank, values[row.par(d)]), (l_bank, None)):
                    for hh in range(HG):
                        k, col = block_place(hh % 2, T - i)
                        ins = pe.matmul(dst[hh * D:(hh + 1) * D, i * P:SEQ],
                                        ones[:] if weights is None else weights[:, i, g * HG + hh, :],
                                        probs[:, g, hh // 2, k, col:col + SEQ - i * P],
                                        start=(i == 0), stop=(i == T - 1))
                ins.then_inc(mix_done, 1)

            def transpose_x(row):
                if row.has(1):
                    n = row.b + 1
                    if row.has(-1):
                        pe.wait_ge(v_done, 2 * (n - 1))
                    else:
                        await_count(pe, qk_split, 4 * n)
                    pe.wait_ge(x_ready, n + 1)
                    for t in range(T):
                        ins = pe.transpose(a_bank[:, t * P:(t + 1) * P],
                                           x2[:, t, :, :].rearrange("p a c -> p (a c)"), ident[:])
                    ins.then_inc(xt_ready, 1)

            def project_qk(row, c):
                if row.has(1):
                    n, g = row.b + 1, c // 2
                    cols = slice((c % 2) * H * D + g * P, (c % 2) * H * D + (g + 1) * P)
                    if c == 0:
                        pe.wait_ge(x_split, n + 1)
                    else:
                        pe.wait_ge(qk_split, 4 * n + c)
                    pe.matmul(a_bank[:], w_hi[:, cols], xs[row.par(1)][:], start=True, stop=False)
                    pe.matmul(a_bank[:], w_lo[:, cols], xs[row.par(1)][:], start=False,
                              stop=True).then_inc(qk_ready, 1)

            def project_v(row, c):
                if row.has(0):
                    if c == 0 and row.has(1):
                        pe.wait_ge(qk_split, 4 * (row.b + 1) + 4)
                    else:
                        await_count(pe, v_done, 2 * row.b + c)
                    for tt in range(2):
                        t = 2 * c + tt
                        for w in (w_hi, w_lo):
                            ins = pe.matmul(a_bank[:, tt * H * D:(tt + 1) * H * D],
                                            xs[row.par(0)][:, t * P:(t + 1) * P], w[:, 2 * H * D:3 * H * D],
                                            start=(w is w_hi), stop=(w is w_lo))
                    ins.then_inc(v_ready, 1)

            def transpose_max(row, d, g):
                if row.has(d):
                    n = row.b + d
                    await_b_bank(pe, row, f"max{g}")
                    pe.wait_ge(nm_split, 2 * n + g + 1)
                    pe.transpose(b_bank[0:2 * HG * T, 0:P],
                                 nm_parts[g][:].bitcast(F32).rearrange("p a n -> p (a n)"),
                                 ident[:]).then_inc(nmt_ready, 1)

            def iteration(row):
                for r in range(STEPS):
                    max_scores(row, r)
                    weight_scores(row, r)
                    if r in MIX:
                        mix(row, *MIX[r])
                    if r == 0:
                        transpose_x(row)
                    if r in A_QK:
                        project_qk(row, A_QK[r])
                    if r in A_V:
                        project_v(row, A_V[r])
                    if r in MAX_ROWS:
                        transpose_max(row, *MAX_ROWS[r])
                    if r == 6 and row.has(-2):
                        n = row.b - 2
                        await_b_bank(pe, row, "y")
                        pe.wait_ge(mixed_done, 2 * n + 2)
                        for t in range(T):
                            for g in range(GROUPS):
                                ins = pe.matmul(b_bank[:, t * C:(t + 1) * C], mixed[g][:, t * P:(t + 1) * P],
                                                wo_sb[:, g, :], start=(g == 0), stop=(g == GROUPS - 1))
                        ins.then_inc(y_ready, 1)
                    if r == 13 and row.has(-2):
                        n = row.b - 2
                        await_b_bank(pe, row, "ft")
                        pe.wait_ge(x2_ready, n + 1)
                        for t in range(T):
                            ins = pe.transpose(b_bank[:, t * P:(t + 1) * P],
                                               ffn_in[:, t, :, :].rearrange("p a c -> p (a c)"), ident[:])
                        ins.then_inc(ft_ready, 1)
                    if r == 16 and row.has(-2):
                        n = row.b - 2
                        await_b_bank(pe, row, "fo")
                        for t in range(T):
                            ins = pe.matmul(b_bank[:, t * C:(t + 1) * C], ffn_in_t[:, t * P:(t + 1) * P],
                                            ffn_rhs[:], start=True, stop=True)
                        ins.then_inc(fo_ready, 1)

            over_rows(pe, iteration)


LOADS = 6 + 1 + 2 + 1 + 1 + 3
CONST_STEPS = 10 + 4 + 2 * H + 2
TABLE_STEPS = 6 + 4 + 7
SETUP_STEPS = TABLE_STEPS + 3

_INS = ["x", "L0_tok_emb1", "L0_tok_emb2", "L0_tok_W", "L0_tok_b", "L0_attn_Wq", "L0_attn_Wk", "L0_attn_Wv",
        "L0_attn_Wo", "L0_attn_bo", "L0_ffn_weight", "L0_ffn_bias"]


def kernel(**inputs):
    import numpy as _np
    import concourse.bacc as _bacc
    from concourse import mybir as _mybir
    from concourse.bass_utils import run_bass_kernel_spmd as _run

    nc = _bacc.Bacc("TRN2", target_bir_lowering=False, num_devices=1)
    arrays, args = {}, []
    for name in _INS:
        a = _np.ascontiguousarray(inputs[name])
        arrays[f"in_{name}_dram"] = a
        args.append(nc.dram_tensor(f"in_{name}_dram", a.shape, _mybir.dt.from_np(a.dtype),
                                   kind="ExternalInput").ap())
    args.append(nc.dram_tensor("out_0_dram", (BATCH, SEQ, C), _mybir.dt.float32, kind="ExternalOutput").ap())
    build(nc, *args)
    r = _run(nc, [arrays], core_ids=[0])
    return r.results[0]["out_0_dram"]
```

```python
from contextlib import ExitStack

import concourse.bass as bass
from concourse import mybir

ALU = mybir.AluOpType
ACT = mybir.ActivationFunctionType
AX_X = mybir.AxisListType.X
F32 = mybir.dt.float32
F32R = mybir.dt.float32r
BF16 = mybir.dt.bfloat16
I32 = mybir.dt.int32

P = 128
BATCH, SEQ, C = 32, 512, 64
CODES = 128
H, D = 8, 32
HG = 4
GROUPS = H // HG
T = SEQ // P
SCALE = float(D) ** -0.5
EPS = 1e-5
SLOPES = [2.0 ** -(h + 1) for h in range(H)]
MASKED = -3.0e38
SHIFT = CODES.bit_length() - 1
QK_ROWS = 3 * D
ALIBI_ROWS = QK_ROWS + 2
ALL_ROWS = ALIBI_ROWS + 2
PAIR_BANKS = 5
UNIT_BANKS = 2 * PAIR_BANKS
STEPS = GROUPS * UNIT_BANKS
LAG = 14
STACK_DMAS = HG * 3
TURN = 4
TURNS = BATCH // TURN
EMBED_AT = {1: (1, 2), 3: (2, 3), 6: (3, 5), 12: (5, 7), 13: (7, TURNS)}
CODE_PARTS = [(1, 3), (3, 5), (5, 7), (7, TURNS)]

PE_JOBS = [(-20, "x", 0), (-17, "qk", 0), (-16, "qk", 1), (-13, "qk", 2), (-10, "qk", 3), (11, "max", 0),
           (12, "v", 0), (17, "v", 1), (21, "max", 1), (27, "mix", 0), (29, "mix", 1), (31, "mix", 2),
           (33, "mix", 3), (38, "mix", 4), (39, "mix", 5), (42, "mix", 6), (43, "mix", 7), (46, "y", 0),
           (54, "ft", 0), (57, "fo", 0)]
ACT_JOBS = [(-26, "rsqrt1", 0), (-19, "x", 0), (-17, "qk", 0), (-15, "qk", 1), (-12, "qk", 2), (-9, "qk", 3),
            (12, "max", 0), (13, "v", 0), (18, "v", 1), (22, "max", 1), (35.5, "norm", 0), (44, "norm", 1),
            (50, "rsqrt2", 0), (55, "ft", 0), (58.5, "fo", 0)]
DVE_JOBS = [(-27.5, "stats", 0), (-18.5, "x", 0), (-16.5, "qk", 0), (-14, "qk", 1), (-12.5, "qk", 2),
            (-8.5, "qk", 3), (10, "max", 0), (20, "max", 1), (37, "norm", 0), (45.5, "norm", 1),
            (46.5, "y", 0)]
POOL_JOBS = [(-21, "ln1", 0), (21, "diagonals", 0), (22, "diagonals", 1), (27, "diagonals", 2),
             (34, "diagonals", 3), (40, "h_bo", 0), (47, "ln2", 0)]


def bank_blocks(k):
    if k == 4:
        return [(0, 2, 0), (1, 2, 2 * P)]
    if k % 2 == 0:
        return [(k // 2, 4, 0)]
    return [(k // 2, 3, 0), (k // 2, 1, 3 * P)]


def block_place(h, extent):
    for k in range(PAIR_BANKS):
        for hh, e, col in bank_blocks(k):
            if hh == h and e == extent:
                return k, col


def build(nc, x, emb1, emb2, tok_w, tok_b, wq, wk, wv, wo, bo, ffn_w, ffn_b, out):
    codes_dram = nc.dram_tensor("codes_scratch", (2, BATCH * SEQ), BF16, kind="Internal").ap()
    out_rows = out.rearrange("b (t p) c -> b p t c", p=P)

    with ExitStack() as ctx:
        def sb(name, shape, dt=F32):
            return ctx.enter_context(nc.sbuf_tensor(name, shape, dt))

        def bank(name, dt=F32):
            return ctx.enter_context(nc.psum_tensor(name, [P, 512], dt))

        def sem(name):
            return ctx.enter_context(nc.semaphore(name))

        h_all = sb("h_all", [P, BATCH, T, C])
        stack = [sb(f"stack{i}", [P, 2, H, SEQ], F32R) for i in range(2)]
        probs = sb("probs", [P, GROUPS, 2, PAIR_BANKS, 512])
        tail = [sb(f"tail{g}", [P, HG, 2 * P]) for g in range(GROUPS)]
        values = [sb(f"values{i}", [P, T, H, D]) for i in range(2)]
        nat = [sb(f"nat{g}", [P, 4, SEQ], F32R) for g in range(GROUPS)]
        xs = [sb(f"xs{i}", [P, SEQ], F32R) for i in range(2)]
        x2 = sb("x2", [P, T, 2, C])
        centred = sb("centred", [P, T, C])
        centred2 = sb("centred2", [P, T, C])
        ffn_in = sb("ffn_in", [P, T, 2, C])
        ffn_in_t = sb("ffn_in_t", [P, SEQ])
        h_bo = sb("h_bo", [P, T, C])
        mixed = [sb(f"mixed{g}", [P, SEQ]) for g in range(GROUPS)]
        log_sum = sb("log_sum", [P, SEQ])
        inv_sum = sb("inv_sum", [P, SEQ])
        out_sb = sb("out_sb", [P, T, C])
        w_hi = sb("w_hi", [P, 3 * H * D], F32R)
        w_lo = sb("w_lo", [P, 3 * H * D], F32R)
        wo_sb = sb("wo_sb", [P, GROUPS, C])
        ffn_rhs = sb("ffn_rhs", [P, C])
        bo_bc = sb("bo_bc", [P, C])
        ffn_b_col = sb("ffn_b_col", [P, 1])
        tok_b_bc = sb("tok_b_bc", [P, C])
        ident = sb("ident", [P, P])
        causal = sb("causal", [P, P], BF16)
        ones = sb("ones", [P, D])
        eps = sb("eps", [P, 1])
        code_id = sb("code_id", [P, 1])
        key_max = [sb(f"key_max{g}", [P, 2, HG, T]) for g in range(GROUPS)]
        row_max = [sb(f"row_max{g}", [P, HG, T]) for g in range(GROUPS)]
        unused = sb("unused", [P, 2, 2, P], BF16)
        nm_parts = [sb(f"nm_parts{g}", [P, 2, HG, T], F32R) for g in range(GROUPS)]
        nm_rows = [sb(f"nm_rows{g}", [2 * HG * T, P], F32R) for g in range(GROUPS)]
        bn1 = sb("bn1", [P, T, 6])
        bn2 = sb("bn2", [P, T, 6])
        mv1 = sb("mv1", [P, T, 2])
        mv2 = sb("mv2", [P, T, 2])
        logv = sb("logv", [P, 2, T])
        rstd1 = sb("rstd1", [P, T])
        rstd2 = sb("rstd2", [P, T])
        tabs = sb("tabs", [P, 2, 3, C], BF16)
        tab_rest = sb("tab_rest", [P, 2, 2, C])
        stage = probs[:, 0, 0, 0:2, :].rearrange("p a c -> p (a c)")[:, 0:3 * H * D]
        pos = probs[:, 0, 0, 2, :]
        emb_in = probs[:, 0, 0, 3, 0:2 * C]
        tokw_in = probs[:, 0, 0, 3, P:2 * P]
        embT = probs[:, 0, 0, 3, 2 * P:3 * P]
        tokwT = probs[:, 0, 0, 3, 3 * P:3 * P + C]
        ffnw_in = probs[:, 0, 0, 4, 0:C]
        coef = probs[:, 0, 0, 4, C:C + 4 * H].rearrange("p (a h) -> p a h", a=4)
        tok = probs[:, 0, 1, 0, 0:P].bitcast(I32)
        tok_code = probs[:, 0, 1, 1, 0:2 * P].bitcast(I32).rearrange("p (e n) -> p e n", e=2)
        tok_f = probs[:, 0, 1, 2, 0:P]
        tok_bf = probs[:, 0, 1, 3, 0:P].bitcast(BF16).rearrange("p (e n) -> p e n", e=2)
        iota_i = probs[:, 0, 1, 4, :].bitcast(I32)
        code_bc = [probs[:, 1, 0, i, :].bitcast(BF16).rearrange("p (e n) -> p e n", e=2) for i in range(TURN)]
        halves = [stack[1][:, side, :, :].rearrange("p h s -> p (h s)").bitcast(BF16)
                  .rearrange("p (e n) -> p e n", e=2) for side in range(2)]
        code_part = [halves[0], halves[1], halves[0],
                     probs[:, 1, 0, 0:TURN, :].rearrange("p k n -> p (k n)").bitcast(BF16)
                     .rearrange("p (e n) -> p e n", e=2)]
        onehot = [probs[:, 1, 1, i, :].bitcast(BF16).rearrange("p (e n) -> p e n", e=2) for i in range(2)]

        m_bank = [bank(f"m_bank{i}") for i in range(2)]
        s_bank = [bank(f"s_bank{i}") for i in range(2)]
        o_bank = bank("o_bank")
        l_bank = bank("l_bank")
        a_bank = bank("a_bank")
        b_bank = bank("b_bank")
        shared = [a_bank, b_bank]

        tables_loaded = sem("tables_loaded")
        loaded = sem("loaded")
        tok_loaded = sem("tok_loaded")
        const = sem("const")
        vconst = sem("vconst")
        pconst = sem("pconst")
        codes_stored = sem("codes_stored")
        code_loaded = [sem(f"code_loaded{i}") for i in range(TURN)]
        part_loaded = [sem(f"part_loaded{i}") for i in range(len(CODE_PARTS))]
        onehot_done = sem("onehot_done")
        bias_copied = sem("bias_copied")
        emb_ready = sem("emb_ready")
        h_done = sem("h_done")
        x_ready = sem("x_ready")
        xt_ready = sem("xt_ready")
        xh_done = sem("xh_done")
        x_split = sem("x_split")
        qk_ready = sem("qk_ready")
        qk_hi = sem("qk_hi")
        qk_split = sem("qk_split")
        stacked = [sem(f"stacked{g}") for g in range(GROUPS)]
        v_ready = sem("v_ready")
        v_done = sem("v_done")
        m_ready = sem("m_ready")
        m_used = sem("m_used")
        max_done = sem("max_done")
        nm_high = sem("nm_high")
        nm_split = sem("nm_split")
        nmt_ready = sem("nmt_ready")
        nm_row = sem("nm_row")
        nm_loaded = [sem(f"nm_loaded{g}") for g in range(GROUPS)]
        s_ready = sem("s_ready")
        exp_done = sem("exp_done")
        masked = sem("masked")
        tail_two = sem("tail_two")
        tail_three = sem("tail_three")
        tail_done = sem("tail_done")
        mix_done = sem("mix_done")
        sum_log = sem("sum_log")
        inv_ready = sem("inv_ready")
        mixed_done = sem("mixed_done")
        h_bo_ready = sem("h_bo_ready")
        y_ready = sem("y_ready")
        res_done = sem("res_done")
        bn2_done = sem("bn2_done")
        mv2_done = sem("mv2_done")
        log2_done = sem("log2_done")
        rstd2_done = sem("rstd2_done")
        cen2_done = sem("cen2_done")
        x2_ready = sem("x2_ready")
        ft_ready = sem("ft_ready")
        ft_done = sem("ft_done")
        fo_ready = sem("fo_ready")
        out_ready = sem("out_ready")
        out_stored = sem("out_stored")
        bn1_done = sem("bn1_done")
        mv1_done = sem("mv1_done")
        log1_done = sem("log1_done")
        rstd1_done = sem("rstd1_done")
        cen1_done = sem("cen1_done")

        held = {e: sem(f"held_{n}") for n, e in (("sp", mybir.EngineType.SP), ("pool", mybir.EngineType.Pool),
                                                 ("dve", mybir.EngineType.DVE))}

        class Row:

            def __init__(self, b, parity, looped):
                self.b, self.parity, self.looped = b, parity, looped

            def has(self, d):
                return self.looped or 0 <= self.b + d < BATCH

            def par(self, d):
                return (self.parity + d) % 2

        def await_count(eng, semaphore, value):
            if not isinstance(value, int) or value > 0:
                eng.wait_ge(semaphore, value)

        def hold(eng):
            eng.sem_inc(held[eng.engine], 1)

        def over_rows(eng, iteration):
            for b in range(4):
                iteration(Row(b, b % 2, False))
            with eng.Fori(2, BATCH // 2 - 1) as pair:
                iteration(Row(2 * pair, 0, True))
                iteration(Row(2 * pair + 1, 1, True))
            for b in range(BATCH - 2, BATCH + 2):
                iteration(Row(b, b % 2, False))

        FILL = [Row(-2, 0, False), Row(-1, 1, False)]

        def embed_turns(eng, row, r, turn_of):
            if row is FILL[1] and r in EMBED_AT:
                with eng.Fori(*EMBED_AT[r]) as turn:
                    for i in range(TURN):
                        turn_of(turn, i, r)

        def row_done(n):
            return n + 1 if isinstance(n, int) else BATCH

        def weight_bank(row, r):
            return (-1, r + STEPS - LAG) if r < LAG else (0, r - LAG)

        def jobs_at(jobs, at):
            return [(-int(step // STEPS), name, c) for step, name, c in jobs if step % STEPS == at]

        READERS = {("x", 0): (x_split, 1, 1), **{("qk", c): (qk_split, 4, c + 1) for c in range(4)},
                   ("v", 0): (v_done, 2, 1), ("v", 1): (v_done, 2, 2), ("max", 0): (nm_row, 2, 1),
                   ("max", 1): (nm_row, 2, 2), ("y", 0): (res_done, 1, 1), ("ft", 0): (ft_done, 1, 1),
                   ("fo", 0): (out_ready, 1, 1)}
        TURNS_TAKEN = sorted(((step % STEPS, -int(step // STEPS), (name, c))
                              for step, name, c in PE_JOBS if (name, c) in READERS), key=lambda entry: entry[0])
        assert len(TURNS_TAKEN) % 2 == 0

        def place_of(job):
            return [entry[2] for entry in TURNS_TAKEN].index(job)

        def bank_of(name, c=0):
            return shared[place_of((name, c)) % 2]

        def await_bank(eng, row, name, c=0):
            for back in range(2, 3 * len(TURNS_TAKEN), 2):
                k = place_of((name, c)) - back
                d = TURNS_TAKEN[k % len(TURNS_TAKEN)][1] + k // len(TURNS_TAKEN)
                if row.has(d):
                    semaphore, per_row, n = READERS[TURNS_TAKEN[k % len(TURNS_TAKEN)][2]]
                    await_count(eng, semaphore, per_row * (row.b + d) + n)
                    return

        block = ctx.enter_context(nc.Block())

        @block.sync
        def _(sp):
            sp.dma_start(tok, x.rearrange("b (q n) -> (b q) n", n=P)).then_inc(tok_loaded, 16)
            sp.dma_start(emb_in[:, 0:C], emb1).then_inc(tables_loaded, 16)
            sp.dma_start(emb_in[:, C:2 * C], emb2).then_inc(tables_loaded, 16)
            sp.dma_start(tokw_in[0:C, :], tok_w).then_inc(tables_loaded, 16)
            with nc.allow_non_contiguous_dma("weights and broadcasts, once"):
                sp.dma_start(tok_b_bc[:], tok_b.partition_broadcast(P)).then_inc(tables_loaded, 16)
                sp.wait_ge(vconst, 6)
                sp.dma_start(codes_dram.rearrange("e (p n) -> p e n", n=P), tok_bf).then_inc(codes_stored, 16)
                sp.wait_ge(codes_stored, 16)

            for i in range(TURN):
                sp.dma_start(code_bc[i], codes_dram[:, i * SEQ:(i + 1) * SEQ].partition_broadcast(P)
                             ).then_inc(code_loaded[i], 16)
            with nc.allow_non_contiguous_dma("weights and broadcasts, once"):
                for half in (0, C):
                    for n, w in enumerate((wq, wk, wv)):
                        sp.dma_start(stage[half:half + C, n * H * D:(n + 1) * H * D], w).then_inc(loaded, 16)
                sp.dma_start(ffnw_in[0:C, :], ffn_w).then_inc(loaded, 16)
                sp.dma_start(wo_sb[:], wo.rearrange("(g p) c -> p g c", p=P)).then_inc(loaded, 16)
                sp.dma_start(ffn_b_col[C:P, :], ffn_b.unsqueeze(1)).then_inc(loaded, 16)
                sp.dma_start(bo_bc[:], bo.partition_broadcast(P)).then_inc(loaded, 16)
            for part, (first, last) in enumerate(CODE_PARTS):
                if part == 2:
                    sp.wait_ge(onehot_done, TURN * CODE_PARTS[0][1])
                if part == 3:
                    sp.wait_ge(onehot_done, TURN)
                sp.dma_start(code_part[part][:, :, 0:(last - first) * TURN * SEQ],
                             codes_dram[:, first * TURN * SEQ:last * TURN * SEQ].partition_broadcast(P)
                             ).then_inc(part_loaded[part], 16)

            def load_max_rows(row, d, g):
                if row.has(d):
                    n = row.b + d
                    sp.wait_ge(nm_row, 2 * n + g + 1)
                    sp.dma_start(stack[row.par(d)][ALIBI_ROWS:ALL_ROWS, 0, g * HG:(g + 1) * HG, :].bitcast(F32),
                                 nm_rows[g][:].bitcast(F32)).then_inc(nm_loaded[g], 16)

            def load_stacks(row, g):
                if row.has(1):
                    n = row.b + 1
                    await_count(sp, s_ready, STEPS * (n - 2) + UNIT_BANKS * (g + 1))
                    hold(sp)
                    sp.wait_ge(qk_split, 4 * n + 2 * g + 2)
                    for j in range(HG):
                        for s, parts in enumerate((slice(0, 3, 2), slice(1, 3), slice(1, 4, 2))):
                            sp.dma_start(stack[row.par(1)][s * D:(s + 1) * D, :, g * HG + j, :].bitcast(F32),
                                         nat[g][j * D:(j + 1) * D, parts, :].bitcast(F32)).then_inc(stacked[g], 16)

            def iteration(row):
                load_max_rows(row, -1, 1)
                load_stacks(row, 0)
                load_max_rows(row, 0, 0)
                load_stacks(row, 1)
                if row.has(-2):
                    n = row.b - 2
                    sp.wait_ge(out_ready, n + 1)
                    sp.dma_start(out_rows[n] if isinstance(n, int) else
                                 out_rows[bass.ds(n, 1)].rearrange("o p t c -> (o p) t c"),
                                 out_sb[:]).then_inc(out_stored, 16)

            for row in FILL:
                iteration(row)
            sp.wait_ge(onehot_done, BATCH)
            sp.wait_ge(const, BIAS_STEPS)
            sp.dma_start(stack[1][QK_ROWS:ALL_ROWS, :, :, :].bitcast(F32),
                         stack[0][QK_ROWS:ALL_ROWS, :, :, :].bitcast(F32)).then_inc(bias_copied, 16)
            over_rows(sp, iteration)
            sp.wait_ge(out_stored, 16 * BATCH)

        @block.gpsimd
        def _(pool):
            count = [0]

            def step(ins):
                count[0] += 1
                ins.then_inc(const, 1)
                pool.wait_ge(const, count[0])

            step(pool.memset(ident[:], 0.0))
            step(pool.affine_select(out=ident[:], in_=ident[:], compare_op=ALU.not_equal, fill=1.0, base=0,
                                    pattern=[[-1, P]], channel_multiplier=1))
            step(pool.iota(code_id[:], pattern=[[0, 1]], base=0, channel_multiplier=1,
                           allow_small_or_imprecise_dtypes=True))
            step(pool.memset(eps[:], EPS))
            step(pool.memset(causal[:], 0.0))
            step(pool.affine_select(out=causal[:], in_=causal[:], compare_op=ALU.is_ge, fill=MASKED, base=0,
                                    pattern=[[-1, P]], channel_multiplier=1))
            step(pool.memset(ones[:], 1.0))
            assert count[0] == CONST_STEPS

            def diagonals(row, d, pair):
                if row.has(d):
                    n = row.b + d
                    g, half = divmod(pair, 2)
                    pool.wait_ge(exp_done, STEPS * n + PAIR_BANKS * (pair + 1))
                    hold(pool)
                    banks = probs[:, g, half, :, :]
                    for part, width in ((banks[:, :, 0:P], 5), (banks[:, 1:4:2, 3 * P:4 * P], 2),
                                        (banks[:, 4:5, 2 * P:3 * P], 1)):
                        ins = pool.affine_select(out=part, in_=part, compare_op=ALU.is_ge, fill=0.0, base=0,
                                                 pattern=[[0, width], [1, P]], channel_multiplier=-1)
                    ins.then_inc(masked, 1)
                    pool.wait_ge(masked, 4 * n + pair + 1)
                    sums = tail[g][:, 2 * half:2 * half + 2, :]
                    pool.tensor_tensor(sums, banks[:, 1:4:2, P:3 * P],
                                       banks[:, 4, :].rearrange("p (h s) -> p h s", h=2), ALU.add).then_inc(tail_two, 1)
                    pool.wait_ge(tail_two, 4 * n + pair + 1)
                    pool.tensor_tensor(sums, sums, banks[:, 0:3:2, 2 * P:4 * P], ALU.add).then_inc(tail_three, 1)
                    pool.wait_ge(tail_three, 4 * n + pair + 1)
                    pool.tensor_tensor(sums[:, :, P:2 * P], sums[:, :, P:2 * P], banks[:, 1:4:2, 3 * P:4 * P],
                                       ALU.add).then_inc(tail_done, 1)

            def add_out_bias(row, d, _):
                if row.has(d):
                    n = row.b + d
                    await_count(pool, res_done, n)
                    pool.wait_ge(h_done, row_done(n))
                    pool.tensor_tensor(h_bo[:], h_all[:, n, :, :] if isinstance(n, int) else
                                       h_all[:, bass.ds(n, 1), :, :].rearrange("p o t c -> p (o t) c"),
                                       bo_bc[:, :].unsqueeze(1).broadcast_to([P, T, C]),
                                       ALU.add).then_inc(h_bo_ready, 1)

            def second_layernorm(row, d, _):
                if row.has(d):
                    n = row.b + d
                    pool.wait_ge(mv2_done, n + 1)
                    pool.tensor_tensor(centred2[:], ffn_in[:, :, 1, :],
                                       mv2[:, :, 0:1].broadcast_to([P, T, C]), ALU.subtract).then_inc(cen2_done, 1)
                    pool.wait_ge(cen2_done, n + 1)
                    pool.wait_ge(rstd2_done, n + 1)
                    await_count(pool, ft_ready, n)
                    pool.tensor_tensor(ffn_in[:, :, 0, :], centred2[:],
                                       rstd2[:, :].unsqueeze(2).broadcast_to([P, T, C]),
                                       ALU.mult).then_inc(x2_ready, 1)

            def first_layernorm(row, d, _):
                if row.has(d):
                    n = row.b + d
                    pool.wait_ge(mv1_done, n + 1)
                    pool.wait_ge(h_done, row_done(n))
                    pool.tensor_tensor(centred[:], h_all[:, n, :, :] if isinstance(n, int) else
                                       h_all[:, bass.ds(n, 1), :, :].rearrange("p o t c -> p (o t) c"),
                                       mv1[:, :, 0:1].broadcast_to([P, T, C]), ALU.subtract).then_inc(cen1_done, 1)
                    pool.wait_ge(cen1_done, n + 1)
                    pool.wait_ge(rstd1_done, n + 1)
                    await_count(pool, xt_ready, n)
                    for copy in range(2):
                        ins = pool.tensor_tensor(x2[:, :, copy, :], centred[:],
                                                 rstd1[:, :].unsqueeze(2).broadcast_to([P, T, C]), ALU.mult)
                    ins.then_inc(x_ready, 1)

            work = {"diagonals": diagonals, "h_bo": add_out_bias, "ln1": first_layernorm, "ln2": second_layernorm}

            def iteration(row):
                for r in range(STEPS):
                    for d, name, c in jobs_at(POOL_JOBS, r):
                        work[name](row, d, c)

            iteration(FILL[0])
            step(pool.iota(iota_i, pattern=[[1, SEQ]], base=0, channel_multiplier=0))
            step(pool.tensor_copy(pos, iota_i))
            for n, (value, row_value, at) in enumerate(
                    [(0.0, None, 1), (0.0, 1.0, 0), (0.0, None, 0), (1.0, 0.0, 0)]):
                step(pool.memset(coef[:, n, :], value))
                if row_value is None:
                    for h in range(H):
                        step(pool.affine_select(out=coef[:, n, h:h + 1], in_=coef[:, n, h:h + 1],
                                                compare_op=ALU.not_equal,
                                                fill=-SLOPES[h] if at else SLOPES[h], base=-(QK_ROWS + at),
                                                pattern=[[0, 1]], channel_multiplier=1))
                else:
                    step(pool.affine_select(out=coef[:, n, :], in_=coef[:, n, :], compare_op=ALU.not_equal,
                                            fill=row_value, base=-(QK_ROWS + at), pattern=[[0, H]],
                                            channel_multiplier=1))
            for side in range(2):
                for h in range(H):
                    step(pool.tensor_scalar(stack[0][QK_ROWS:ALL_ROWS, side, h, :], pos[QK_ROWS:ALL_ROWS, :],
                                            coef[QK_ROWS:ALL_ROWS, 2 * side, h:h + 1],
                                            coef[QK_ROWS:ALL_ROWS, 2 * side + 1, h:h + 1], ALU.mult, ALU.add))
            assert count[0] == BIAS_STEPS
            iteration(FILL[1])
            over_rows(pool, iteration)

        @block.scalar
        def _(act):
            def tanh_row(turn, i, _=None):
                b = TURN * turn + i
                act.wait_ge(emb_ready, b + 1)
                dst = (h_all[:, b, :, :].rearrange("p t c -> p (t c)") if isinstance(b, int) else
                       h_all[:, bass.ds(b, 1), :, :].rearrange("p o t c -> p (o t c)"))
                act.activation(dst, m_bank[i % 2][:, 0:T * C], ACT.Tanh).then_inc(h_done, 1)

            act.preload_act_table_set("exp_and_others")
            act.wait_ge(const, CONST_STEPS)
            for i in range(TURN):
                tanh_row(0, i)

            def exp_bank(row, r):
                d, idx = weight_bank(row, r)
                if not row.has(d):
                    return
                n, g = row.b + d, idx // UNIT_BANKS
                half, k = divmod(idx % UNIT_BANKS, PAIR_BANKS)
                if idx % UNIT_BANKS == 0:
                    await_count(act, mix_done, 8 * (n - 1) + 4 * g + 4)
                act.wait_ge(s_ready, STEPS * n + idx + 1)
                act.activation(probs[:, g, half, k, :], s_bank[idx % 2][:], ACT.Exp).then_inc(exp_done, 1)

            def x_high(row, d, _):
                if row.has(d):
                    n = row.b + d
                    act.wait_ge(xt_ready, n + 1)
                    await_count(act, v_ready, 2 * (n - 2) + 2)
                    act.copy(xs[row.par(d)][:], bank_of("x")[:]).then_inc(xh_done, 1)

            def qk_high(row, d, c):
                if row.has(d):
                    n, g = row.b + d, c // 2
                    await_count(act, stacked[g], 16 * STACK_DMAS * n)
                    act.wait_ge(qk_ready, 4 * n + c + 1)
                    if c % 2 == 0:
                        ins = act.mul(nat[g][:, 1, :], bank_of("qk", c)[:], SCALE)
                    else:
                        ins = act.copy(nat[g][:, 2, :], bank_of("qk", c)[:])
                    ins.then_inc(qk_hi, 1)

            def copy_values(row, d, c):
                if row.has(d):
                    n = row.b + d
                    await_count(act, mix_done, 8 * (n - 2) + 8)
                    act.wait_ge(v_ready, 2 * n + c + 1)
                    act.copy(values[row.par(d)][:, 2 * c:2 * c + 2, :, :],
                             bank_of("v", c)[:].rearrange("p (t h d) -> p t h d", t=2, h=H)).then_inc(v_done, 1)

            def copy_max_rows(row, d, g):
                if row.has(d):
                    n = row.b + d
                    await_count(act, nm_loaded[g], 16 * n)
                    act.wait_ge(nmt_ready, 2 * n + g + 1)
                    act.copy(nm_rows[g][:], bank_of("max", g)[0:2 * HG * T, 0:P]).then_inc(nm_row, 1)

            def invert_sums(row, d, g):
                if row.has(d):
                    n = row.b + d
                    act.wait_ge(mix_done, 8 * n + 4 * g + 4)
                    act.activation(log_sum[:], l_bank[:], ACT.Ln).then_inc(sum_log, 1)
                    await_count(act, mixed_done, 2 * n + g)
                    act.wait_ge(sum_log, 2 * n + g + 1)
                    act.activation(inv_sum[:], log_sum[:], ACT.Exp, scale=-1.0).then_inc(inv_ready, 1)

            def rsqrt(n, which, mv, mv_done, log_done, rstd, rstd_used, rstd_done):
                act.wait_ge(mv_done, n + 1)
                act.activation(logv[:, which, :].unsqueeze(2), mv[:, :, 1:2], ACT.Ln,
                               bias=eps[:, 0:1]).then_inc(log_done, 1)
                await_count(act, rstd_used, n)
                act.wait_ge(log_done, n + 1)
                act.activation(rstd[:], logv[:, which, :], ACT.Exp, scale=-0.5).then_inc(rstd_done, 1)

            def rsqrt_first(row, d, _):
                if row.has(d):
                    rsqrt(row.b + d, 0, mv1, mv1_done, log1_done, rstd1, x_ready, rstd1_done)

            def rsqrt_second(row, d, _):
                if row.has(d):
                    rsqrt(row.b + d, 1, mv2, mv2_done, log2_done, rstd2, x2_ready, rstd2_done)

            def copy_ffn_in(row, d, _):
                if row.has(d):
                    n = row.b + d
                    await_count(act, fo_ready, n)
                    act.wait_ge(ft_ready, n + 1)
                    act.activation(ffn_in_t[:], bank_of("ft")[:], ACT.Identity, bias=ffn_b_col[:, 0:1]).then_inc(ft_done, 1)

            def copy_out(row, d, _):
                if row.has(d):
                    n = row.b + d
                    await_count(act, out_stored, 16 * n)
                    act.wait_ge(fo_ready, n + 1)
                    act.copy(out_sb[:], bank_of("fo")[:, 0:T * C].rearrange("p (t c) -> p t c", t=T)).then_inc(out_ready, 1)

            work = {"rsqrt1": rsqrt_first, "x": x_high, "qk": qk_high, "v": copy_values, "max": copy_max_rows,
                    "norm": invert_sums, "rsqrt2": rsqrt_second, "ft": copy_ffn_in, "fo": copy_out}

            def iteration(row):
                for r in range(STEPS):
                    embed_turns(act, row, r, tanh_row)
                    if row is FILL[1] and r == max(EMBED_AT):
                        act.preload_act_table_set("natural_log_exp_and_others")
                    for d, name, c in jobs_at(ACT_JOBS, r):
                        work[name](row, d, c)
                    exp_bank(row, r)
                    for d, name, c in jobs_at(ACT_JOBS, r + 0.5):
                        work[name](row, d, c)

            act.preload_act_table_set("natural_log_exp_and_others")
            iteration(FILL[0])
            act.preload_act_table_set("exp_and_others")
            iteration(FILL[1])
            over_rows(act, iteration)

        @block.vector
        def _(dve):
            count = [0]

            def step(ins):
                count[0] += 1
                ins.then_inc(vconst, 1)
                dve.wait_ge(vconst, count[0])

            dve.wait_ge(tok_loaded, 16)
            step(dve.tensor_scalar(tok_code[:, 0, :], tok, SHIFT, None, ALU.arith_shift_right))
            step(dve.tensor_scalar(tok_code[:, 1, :], tok, CODES - 1, None, ALU.bitwise_and))
            step(dve.tensor_copy(tok_f, tok_code[:, 0, :]))
            step(dve.tensor_scalar(tok_f, tok_f, 0.0, float(CODES - 1), ALU.max, ALU.min))
            step(dve.tensor_copy(tok_bf[:, 0, :], tok_f))
            step(dve.tensor_copy(tok_bf[:, 1, :], tok_code[:, 1, :]))

            dve.wait_ge(tables_loaded, 16 * TABLE_LOADS)
            dve.wait_ge(pconst, 1)
            dve.tensor_copy(embT, a_bank[:, 0:P]).then_inc(vconst, 1)
            dve.tensor_copy(tokwT, a_bank[:, P:P + C]).then_inc(vconst, 1)
            count[0] += 2
            dve.wait_ge(pconst, 3)
            step(dve.tensor_tensor(tab_rest[:, 0, 0, :], b_bank[:, 0:C], tok_b_bc[:], ALU.add))
            step(dve.tensor_copy(tab_rest[:, 1, 0, :], o_bank[:, 0:C]))
            step(dve.tensor_copy(tabs[:, :, 0, :], tab_rest[:, :, 0, :]))
            step(dve.tensor_tensor(tab_rest[:, :, 1, :], tab_rest[:, :, 0, :], tabs[:, :, 0, :], ALU.subtract))
            step(dve.tensor_copy(tabs[:, :, 1, :], tab_rest[:, :, 1, :]))
            step(dve.tensor_tensor(tab_rest[:, :, 0, :], tab_rest[:, :, 1, :], tabs[:, :, 1, :], ALU.subtract))
            step(dve.tensor_copy(tabs[:, :, 2, :], tab_rest[:, :, 0, :]))
            assert count[0] == TABLE_STEPS

            dve.wait_ge(const, CONST_STEPS)

            def one_hot(turn, i, r=None):
                b = TURN * turn + i
                if r is None:
                    codes = code_bc[i]
                    dve.wait_ge(code_loaded[i], 16)
                else:
                    part = [first <= EMBED_AT[r][0] < last for first, last in CODE_PARTS].index(True)
                    codes = code_part[part][:, :, bass.ds((b - TURN * CODE_PARTS[part][0]) * SEQ, SEQ)]
                    dve.wait_ge(part_loaded[part], 16)
                await_count(dve, emb_ready, b - 1)
                dve.tensor_scalar(onehot[i % 2], codes, code_id[:, 0:1], None,
                                  ALU.is_equal).then_inc(onehot_done, 1)

            for i in range(TURN):
                one_hot(0, i)

            dve.wait_ge(loaded, 16 * LOADS)
            step(dve.tensor_copy(w_hi[:], stage))
            step(dve.tensor_tensor(w_lo[:], stage, w_hi[:].bitcast(F32), ALU.subtract))
            step(dve.tensor_copy(ffn_rhs[C:P, :], ident[C:P, C:P]))
            dve.wait_ge(pconst, 4)
            step(dve.tensor_copy(ffn_rhs[0:C, :], a_bank[0:C, 2 * P:2 * P + C]))
            dve.memset(ffn_b_col[0:C, :], 0.0)
            for g in range(GROUPS):
                ins = dve.memset(key_max[g][:, 0, :, 0:1], MASKED)
            step(ins)
            assert count[0] == SETUP_STEPS

            def maxima(row, r):
                if not row.has(0):
                    return
                g, idx = divmod(r, UNIT_BANKS)
                half, k = divmod(idx, PAIR_BANKS)
                src = m_bank[r % 2]
                full, diagonal = key_max[g][:, 0, :, :], key_max[g][:, 1, :, :]
                dve.wait_ge(m_ready, STEPS * row.b + r + 1)
                if k == 4:
                    dve.tensor_reduce(full[:, 2 * half:2 * half + 2, 1:2],
                                      src[:].rearrange("p (h s) -> p h s", h=2)[:, :, 0:P], AX_X, ALU.max)
                else:
                    h, extent, col = bank_blocks(k)[0]
                    dve.tensor_reduce(full[:, 2 * half + h, extent - 1:extent],
                                      src[:, col:col + (extent - 1) * P], AX_X, ALU.max)
                for h, extent, col in bank_blocks(k):
                    diag = col + (extent - 1) * P
                    ins = dve.tensor_tensor_reduce(out=unused[:, r % 2, h, :] if k == 4 else unused[:, r % 2, int(extent == 1), :],
                                                   in0=src[:, diag:diag + P], in1=causal[:],
                                                   scale=1.0, scalar=MASKED, op0=ALU.add, op1=ALU.max,
                                                   accum_out=diagonal[:, 2 * half + h, extent - 1:extent])
                ins.then_inc(m_used, 1)

            def split_max(row, d, g):
                if row.has(d):
                    n = row.b + d
                    await_count(dve, nmt_ready, 2 * (n - 1) + g + 1)
                    dve.wait_ge(m_used, STEPS * n + UNIT_BANKS * (g + 1))
                    dve.tensor_tensor(row_max[g][:], key_max[g][:, 0, :, :], key_max[g][:, 1, :, :],
                                      ALU.max).then_inc(max_done, 1)
                    dve.wait_ge(max_done, 2 * n + g + 1)
                    dve.tensor_scalar(nm_parts[g][:, 0, :, :], row_max[g][:], -1.0, None,
                                      ALU.mult).then_inc(nm_high, 1)
                    dve.wait_ge(nm_high, 2 * n + g + 1)
                    dve.scalar_tensor_tensor(out=nm_parts[g][:, 1, :, :], in0=row_max[g][:], scalar=-1.0,
                                             in1=nm_parts[g][:, 0, :, :].bitcast(F32), op0=ALU.mult,
                                             op1=ALU.subtract).then_inc(nm_split, 1)

            def x_low(row, d, _):
                if row.has(d):
                    n = row.b + d
                    lo = xs[row.par(d)][C:P, :]
                    dve.wait_ge(xh_done, n + 1)
                    dve.tensor_tensor(lo, bank_of("x")[C:P, :], lo.bitcast(F32), ALU.subtract).then_inc(x_split, 1)

            def qk_low(row, d, c):
                if row.has(d):
                    n, g = row.b + d, c // 2
                    dve.wait_ge(qk_hi, 4 * n + c + 1)
                    if c % 2 == 0:
                        ins = dve.scalar_tensor_tensor(out=nat[g][:, 0, :], in0=bank_of("qk", c)[:], scalar=SCALE,
                                                       in1=nat[g][:, 1, :].bitcast(F32), op0=ALU.mult,
                                                       op1=ALU.subtract)
                    else:
                        ins = dve.tensor_tensor(nat[g][:, 3, :], bank_of("qk", c)[:], nat[g][:, 2, :].bitcast(F32),
                                                ALU.subtract)
                    ins.then_inc(qk_split, 1)

            def normalise(row, d, g):
                if row.has(d):
                    n = row.b + d
                    await_count(dve, y_ready, n)
                    dve.wait_ge(inv_ready, 2 * n + g + 1)
                    dve.tensor_tensor(mixed[g][:], o_bank[:], inv_sum[:], ALU.mult).then_inc(mixed_done, 1)

            def residual(row, d, _):
                if row.has(d):
                    n = row.b + d
                    dve.wait_ge(h_bo_ready, n + 1)
                    await_count(dve, ft_ready, n)
                    dve.wait_ge(y_ready, n + 1)
                    dve.tensor_tensor(ffn_in[:, :, 1, :], bank_of("y")[:, 0:T * C].rearrange("p (t c) -> p t c", t=T),
                                      h_bo[:], ALU.add).then_inc(res_done, 1)
                    dve.wait_ge(res_done, n + 1)
                    for t in range(T):
                        ins = dve.bn_stats(bn2[:, t, :], ffn_in[:, t, 1, :])
                    ins.then_inc(bn2_done, 1)
                    dve.wait_ge(bn2_done, n + 1)
                    await_count(dve, rstd2_done, n)
                    await_count(dve, x2_ready, n)
                    hold(dve)
                    for t in range(T):
                        ins = dve.bn_aggr(mv2[:, t, :], bn2[:, t, :])
                    ins.then_inc(mv2_done, 1)

            def statistics(row, d, _):
                if row.has(d):
                    n = row.b + d
                    for t in range(T):
                        src = (h_all[:, n, t, :] if isinstance(n, int) else
                               h_all[:, bass.ds(n, 1), t, :].rearrange("p o c -> p (o c)"))
                        if t == 0:
                            dve.wait_ge(h_done, row_done(n))
                        ins = dve.bn_stats(bn1[:, t, :], src)
                    ins.then_inc(bn1_done, 1)
                    dve.wait_ge(bn1_done, n + 1)
                    await_count(dve, rstd1_done, n)
                    await_count(dve, cen1_done, n)
                    hold(dve)
                    for t in range(T):
                        ins = dve.bn_aggr(mv1[:, t, :], bn1[:, t, :])
                    ins.then_inc(mv1_done, 1)

            work = {"stats": statistics, "x": x_low, "qk": qk_low, "max": split_max, "norm": normalise,
                    "y": residual}

            def iteration(row):
                for r in range(STEPS):
                    embed_turns(dve, row, r, one_hot)
                    for d, name, c in jobs_at(DVE_JOBS, r):
                        work[name](row, d, c)
                    maxima(row, r)
                    for d, name, c in jobs_at(DVE_JOBS, r + 0.5):
                        work[name](row, d, c)

            for row in FILL:
                iteration(row)
            over_rows(dve, iteration)

        @block.tensor
        def _(pe):
            pe.wait_ge(const, CONST_STEPS)
            pe.wait_ge(tables_loaded, 16 * TABLE_LOADS)
            pe.transpose(a_bank[:, 0:P], emb_in, ident[:])
            pe.transpose(a_bank[:, P:P + C], tokw_in[0:C, :], ident[0:C, 0:C]).then_inc(pconst, 1)
            pe.wait_ge(vconst, 8)
            pe.matmul(b_bank[:, 0:C], embT[0:C, :], tokwT[0:C, :], start=True, stop=True).then_inc(pconst, 1)
            pe.matmul(o_bank[:, 0:C], embT[C:P, :], tokwT[C:P, :], start=True, stop=True).then_inc(pconst, 1)
            pe.wait_ge(vconst, TABLE_STEPS)

            def embed(turn, i, _=None):
                b = TURN * turn + i
                pe.wait_ge(onehot_done, b + 1)
                await_count(pe, h_done, b - 1)
                for t in range(T):
                    for e in range(2):
                        for part in range(3):
                            ins = pe.matmul(m_bank[i % 2][:, t * C:(t + 1) * C],
                                            onehot[i % 2][:, e, t * P:(t + 1) * P], tabs[:, e, part, :],
                                            start=(e == 0 and part == 0), stop=(e == 1 and part == 2))
                ins.then_inc(emb_ready, 1)

            for i in range(TURN):
                embed(0, i)
            pe.wait_ge(loaded, 16 * LOADS)
            pe.transpose(a_bank[0:C, 2 * P:2 * P + C], ffnw_in[0:C, :], ident[0:C, 0:C]).then_inc(pconst, 1)
            pe.wait_ge(vconst, SETUP_STEPS)

            def max_scores(row, r):
                if not row.has(0):
                    return
                g, idx = divmod(r, UNIT_BANKS)
                half, k = divmod(idx, PAIR_BANKS)
                st, dst = stack[row.par(0)], m_bank[r % 2]
                if idx == 0:
                    pe.wait_ge(stacked[g], 16 * STACK_DMAS * (row.b + 1))
                await_count(pe, m_used, STEPS * row.b + r - 1)
                for hh, extent, col in bank_blocks(k):
                    head, diag = g * HG + 2 * half + hh, (extent - 1) * P
                    ins = pe.matmul(dst[:, col:col + extent * P], st[0:ALIBI_ROWS, 0, head, diag:diag + P],
                                    st[0:ALIBI_ROWS, 1, head, 0:extent * P], start=True, stop=True)
                ins.then_inc(m_ready, 1)

            def weight_scores(row, r):
                d, index = weight_bank(row, r)
                if not row.has(d):
                    return
                n = row.b + d
                g, idx = divmod(index, UNIT_BANKS)
                half, k = divmod(idx, PAIR_BANKS)
                st, dst = stack[row.par(d)], s_bank[index % 2]
                if idx == 0:
                    pe.wait_ge(nm_loaded[g], 16 * (n + 1))
                await_count(pe, exp_done, STEPS * n + index - 1)
                for hh, extent, col in bank_blocks(k):
                    head, first = g * HG + 2 * half + hh, SEQ - extent * P
                    ins = pe.matmul(dst[:, col:col + extent * P], st[0:ALL_ROWS, 1, head, first:first + P],
                                    st[0:ALL_ROWS, 0, head, first:SEQ], start=True, stop=True)
                ins.then_inc(s_ready, 1)

            def mix(row, d, c):
                if not row.has(d):
                    return
                n = row.b + d
                g, i = divmod(c, T)
                if i == 0:
                    pe.wait_ge(masked, 4 * n + 2 * g + 2)
                    pe.wait_ge(v_done, 2 * n + 2)
                    await_count(pe, sum_log, 2 * n + g)
                    await_count(pe, mixed_done, 2 * n + g)
                for hh in range(HG):
                    k, col = block_place(hh % 2, T - i)
                    ins = pe.matmul(o_bank[hh * D:(hh + 1) * D, i * P:SEQ], values[row.par(d)][:, i, g * HG + hh, :],
                                    probs[:, g, hh // 2, k, col:col + SEQ - i * P],
                                    start=(i == 0), stop=(i == T - 1))
                if i == T - 1:
                    pe.wait_ge(tail_done, 4 * n + 2 * g + 2)
                for hh in range(HG):
                    k, col = block_place(hh % 2, T - i)
                    if i == 0:
                        first, last, weights = 0, 2 * P, probs[:, g, hh // 2, k, col:col + 2 * P]
                    elif i == 1:
                        first, last, weights = P, 2 * P, probs[:, g, hh // 2, k, col:col + P]
                    elif i == T - 1:
                        first, last, weights = 2 * P, SEQ, tail[g][:, hh, :]
                    else:
                        continue
                    ins = pe.matmul(l_bank[hh * D:(hh + 1) * D, first:last], ones[:], weights,
                                    start=(i != 1), stop=(i != 0), skip_group_check=True)
                ins.then_inc(mix_done, 1)

            def transpose_x(row, d, _):
                if row.has(d):
                    n = row.b + d
                    await_bank(pe, row, "x")
                    pe.wait_ge(x_ready, n + 1)
                    for t in range(T):
                        ins = pe.transpose(bank_of("x")[:, t * P:(t + 1) * P],
                                           x2[:, t, :, :].rearrange("p a c -> p (a c)"), ident[:])
                    ins.then_inc(xt_ready, 1)

            def project_qk(row, d, c):
                if row.has(d):
                    n, g = row.b + d, c // 2
                    cols = slice((c % 2) * H * D + g * P, (c % 2) * H * D + (g + 1) * P)
                    await_bank(pe, row, "qk", c)
                    if c == 0:
                        pe.wait_ge(x_split, n + 1)
                    pe.matmul(bank_of("qk", c)[:], w_hi[:, cols], xs[row.par(d)][:], start=True, stop=False)
                    pe.matmul(bank_of("qk", c)[:], w_lo[:, cols], xs[row.par(d)][:], start=False,
                              stop=True).then_inc(qk_ready, 1)

            def project_v(row, d, c):
                if row.has(d):
                    n = row.b + d
                    await_bank(pe, row, "v", c)
                    for tt in range(2):
                        t = 2 * c + tt
                        for w in (w_hi, w_lo):
                            ins = pe.matmul(bank_of("v", c)[:, tt * H * D:(tt + 1) * H * D],
                                            xs[row.par(d)][:, t * P:(t + 1) * P], w[:, 2 * H * D:3 * H * D],
                                            start=(w is w_hi), stop=(w is w_lo))
                    ins.then_inc(v_ready, 1)

            def transpose_max(row, d, g):
                if row.has(d):
                    n = row.b + d
                    await_bank(pe, row, "max", g)
                    pe.wait_ge(nm_split, 2 * n + g + 1)
                    pe.transpose(bank_of("max", g)[0:2 * HG * T, 0:P],
                                 nm_parts[g][:].bitcast(F32).rearrange("p a h t -> p (a h t)"),
                                 ident[:]).then_inc(nmt_ready, 1)

            def project_out(row, d, _):
                if row.has(d):
                    n = row.b + d
                    await_bank(pe, row, "y")
                    pe.wait_ge(mixed_done, 2 * n + 2)
                    for t in range(T):
                        for g in range(GROUPS):
                            ins = pe.matmul(bank_of("y")[:, t * C:(t + 1) * C], mixed[g][:, t * P:(t + 1) * P],
                                            wo_sb[:, g, :], start=(g == 0), stop=(g == GROUPS - 1))
                    ins.then_inc(y_ready, 1)

            def transpose_ffn_in(row, d, _):
                if row.has(d):
                    n = row.b + d
                    await_bank(pe, row, "ft")
                    pe.wait_ge(x2_ready, n + 1)
                    for t in range(T):
                        ins = pe.transpose(bank_of("ft")[:, t * P:(t + 1) * P],
                                           ffn_in[:, t, :, :].rearrange("p a c -> p (a c)"), ident[:])
                    ins.then_inc(ft_ready, 1)

            def feed_forward(row, d, _):
                if row.has(d):
                    await_bank(pe, row, "fo")
                    pe.wait_ge(ft_done, row.b + d + 1)
                    for t in range(T):
                        ins = pe.matmul(bank_of("fo")[:, t * C:(t + 1) * C], ffn_in_t[:, t * P:(t + 1) * P],
                                        ffn_rhs[:], start=True, stop=True)
                    ins.then_inc(fo_ready, 1)

            work = {"x": transpose_x, "qk": project_qk, "v": project_v, "max": transpose_max, "mix": mix,
                    "y": project_out, "ft": transpose_ffn_in, "fo": feed_forward}

            def iteration(row):
                for r in range(STEPS):
                    embed_turns(pe, row, r, embed)
                    max_scores(row, r)
                    weight_scores(row, r)
                    for d, name, c in jobs_at(PE_JOBS, r):
                        work[name](row, d, c)

            for row in FILL:
                iteration(row)
            pe.wait_ge(h_done, BATCH)
            pe.wait_ge(const, BIAS_STEPS)
            pe.wait_ge(bias_copied, 16)
            over_rows(pe, iteration)


TABLE_LOADS = 4
LOADS = 6 + 4
CONST_STEPS = 7
BIAS_STEPS = CONST_STEPS + 2 + 4 + 2 * H + 2 + 2 * H
TABLE_STEPS = 6 + 2 + 7
SETUP_STEPS = TABLE_STEPS + 5

_INS = ["x", "L0_tok_emb1", "L0_tok_emb2", "L0_tok_W", "L0_tok_b", "L0_attn_Wq", "L0_attn_Wk", "L0_attn_Wv",
        "L0_attn_Wo", "L0_attn_bo", "L0_ffn_weight", "L0_ffn_bias"]


def kernel(**inputs):
    import numpy as _np
    import concourse.bacc as _bacc
    from concourse import mybir as _mybir
    from concourse.bass_utils import run_bass_kernel_spmd as _run

    nc = _bacc.Bacc("TRN2", target_bir_lowering=False, num_devices=1)
    arrays, args = {}, []
    for name in _INS:
        a = _np.ascontiguousarray(inputs[name])
        arrays[f"in_{name}_dram"] = a
        args.append(nc.dram_tensor(f"in_{name}_dram", a.shape, _mybir.dt.from_np(a.dtype),
                                   kind="ExternalInput").ap())
    args.append(nc.dram_tensor("out_0_dram", (BATCH, SEQ, C), _mybir.dt.float32, kind="ExternalOutput").ap())
    build(nc, *args)
    r = _run(nc, [arrays], core_ids=[0])
    return r.results[0]["out_0_dram"]
```

```python
from contextlib import ExitStack

import concourse.bass as bass
from concourse import mybir

ALU = mybir.AluOpType
ACT = mybir.ActivationFunctionType
AX_X = mybir.AxisListType.X
F32 = mybir.dt.float32
F32R = mybir.dt.float32r
BF16 = mybir.dt.bfloat16
I32 = mybir.dt.int32

P = 128
BATCH, SEQ, C = 32, 512, 64
CODES = 128
H, D = 8, 32
HG = 4
GROUPS = H // HG
T = SEQ // P
SCALE = float(D) ** -0.5
EPS = 1e-5
SLOPES = [2.0 ** -(h + 1) for h in range(H)]
MASKED = -3.0e38
SHIFT = CODES.bit_length() - 1
QK_ROWS = 3 * D
ALIBI_ROWS = QK_ROWS + 2
ALL_ROWS = ALIBI_ROWS + 2
PAIR_BANKS = 5
UNIT_BANKS = 2 * PAIR_BANKS
STEPS = GROUPS * UNIT_BANKS
LAG = 16
STACK_DMAS = HG * 3
TURN = 4
TURNS = BATCH // TURN
EMBED_AT = {2: (1, 3), 5: (3, 5), 12: (5, 7), 14: (7, TURNS)}
CODE_PARTS = [(1, 3), (3, 5), (5, 7), (7, TURNS)]

PE_JOBS = [(-20, "x", 0), (-17, "qk", 0), (-17, "qk", 1), (-15, "qk", 2), (-10, "qk", 3), (11, "max", 0),
           (13, "v", 0), (16, "v", 1), (21, "max", 1), (29, "mix", 0), (29, "mix", 1), (32, "mix", 2),
           (33, "mix", 3), (38, "mix", 4), (39, "mix", 5), (42, "mix", 6), (44, "mix", 7), (47, "y", 0),
           (54, "ft", 0), (57, "fo", 0)]
ACT_JOBS = [(-26, "rsqrt1", 0), (-21.5, "apply1", 0), (-21.5, "apply1", 1), (-19.5, "x", 0), (-17, "qk", 0),
            (-16, "qk", 1), (-13.5, "qk", 2), (-9, "qk", 3), (12.5, "max", 0), (14, "v", 0), (17, "v", 1),
            (22, "max", 1), (35.5, "log", 0), (35.5, "norm", 0), (44, "log", 1), (44, "norm", 1),
            (50, "rsqrt2", 0), (53, "apply2", 0), (53, "apply2", 1), (55, "ft", 0), (58.5, "fo", 0)]
DVE_JOBS = [(-28, "bn1", 0), (-27, "moments1", 0), (-25, "shift1", 0), (-18.5, "x", 0), (-16.5, "qk", 0),
            (-14.5, "qk", 1), (-12.5, "qk", 2), (-8.5, "qk", 3), (10, "max", 0), (20, "max", 1),
            (22.5, "tails", 0), (26.5, "tails", 1), (31.5, "tails", 2), (37.5, "norm", 0), (38, "tails", 3),
            (45.5, "norm", 1), (47.5, "y", 0), (47.5, "bn2", 0), (49.5, "moments2", 0), (51, "shift2", 0)]
POOL_JOBS = [(21, "diagonals", 0), (22, "diagonals", 1), (23, "diagonals", 2), (37, "diagonals", 3),
             (40, "h_bo", 0)]


def bank_blocks(k):
    if k == 4:
        return [(0, 2, 0), (1, 2, 2 * P)]
    if k % 2 == 0:
        return [(k // 2, 4, 0)]
    return [(k // 2, 3, 0), (k // 2, 1, 3 * P)]


def block_place(h, extent):
    for k in range(PAIR_BANKS):
        for hh, e, col in bank_blocks(k):
            if hh == h and e == extent:
                return k, col


def build(nc, x, emb1, emb2, tok_w, tok_b, wq, wk, wv, wo, bo, ffn_w, ffn_b, out):
    codes_dram = nc.dram_tensor("codes_scratch", (2, BATCH * SEQ), BF16, kind="Internal").ap()
    out_rows = out.rearrange("b (t p) c -> b p t c", p=P)

    with ExitStack() as ctx:
        def sb(name, shape, dt=F32):
            return ctx.enter_context(nc.sbuf_tensor(name, shape, dt))

        def bank(name, dt=F32):
            return ctx.enter_context(nc.psum_tensor(name, [P, 512], dt))

        def sem(name):
            return ctx.enter_context(nc.semaphore(name))

        h_all = sb("h_all", [P, BATCH, T, C])
        stack = [sb(f"stack{i}", [P, 2, H, SEQ], F32R) for i in range(2)]
        probs = sb("probs", [P, GROUPS, 2, PAIR_BANKS, 512])
        tail = [sb(f"tail{g}", [P, HG, 3 * P]) for g in range(GROUPS)]
        values = [sb(f"values{i}", [P, T, H, D]) for i in range(2)]
        nat = [sb(f"nat{g}", [P, 4, SEQ], F32R) for g in range(GROUPS)]
        xs = [sb(f"xs{i}", [P, SEQ], F32R) for i in range(2)]
        x2 = sb("x2", [P, T, 2, C])
        ffn_in = sb("ffn_in", [P, T, 2, C])
        ffn_in_t = sb("ffn_in_t", [P, SEQ])
        h_bo = sb("h_bo", [P, T, C])
        mixed = [sb(f"mixed{g}", [P, SEQ]) for g in range(GROUPS)]
        log_sum = sb("log_sum", [P, SEQ])
        inv_sum = sb("inv_sum", [P, SEQ])
        out_sb = sb("out_sb", [P, T, C])
        w_hi = sb("w_hi", [P, 3 * H * D], F32R)
        w_lo = sb("w_lo", [P, 3 * H * D], F32R)
        wo_sb = sb("wo_sb", [P, GROUPS, C])
        ffn_rhs = sb("ffn_rhs", [P, C])
        bo_bc = sb("bo_bc", [P, C])
        ffn_b_col = sb("ffn_b_col", [P, 1])
        tok_b_bc = sb("tok_b_bc", [P, C])
        ident = sb("ident", [P, P])
        causal = sb("causal", [P, SEQ], BF16)
        ones = sb("ones", [P, D])
        eps = sb("eps", [P, 1])
        code_id = sb("code_id", [P, 1])
        row_max = [sb(f"row_max{g}", [P, HG, T]) for g in range(GROUPS)]
        unused = sb("unused", [P, 2, SEQ], BF16)
        nm_parts = [sb(f"nm_parts{g}", [P, 2, HG, T], F32R) for g in range(GROUPS)]
        nm_rows = [sb(f"nm_rows{g}", [2 * HG * T, P], F32R) for g in range(GROUPS)]
        bn1 = sb("bn1", [P, T, 6])
        bn2 = sb("bn2", [P, T, 6])
        mv1 = sb("mv1", [P, T, 2])
        mv2 = sb("mv2", [P, T, 2])
        logv = sb("logv", [P, 2, T])
        rstd1 = sb("rstd1", [P, T])
        rstd2 = sb("rstd2", [P, T])
        shift1 = sb("shift1", [P, T])
        shift2 = sb("shift2", [P, T])
        tabs = sb("tabs", [P, 2, 3, C], BF16)
        tab_rest = sb("tab_rest", [P, 2, 2, C])
        stage = probs[:, 0, 0, 0:2, :].rearrange("p a c -> p (a c)")[:, 0:3 * H * D]
        pos = probs[:, 0, 0, 2, :]
        emb_in = probs[:, 0, 0, 3, 0:2 * C]
        tokw_in = probs[:, 0, 0, 3, P:2 * P]
        embT = probs[:, 0, 0, 3, 2 * P:3 * P]
        tokwT = probs[:, 0, 0, 3, 3 * P:3 * P + C]
        ffnw_in = probs[:, 0, 0, 4, 0:C]
        coef = probs[:, 0, 0, 4, C:C + 4 * H].rearrange("p (a h) -> p a h", a=4)
        tok = probs[:, 0, 1, 0, 0:P].bitcast(I32)
        tok_code = probs[:, 0, 1, 1, 0:2 * P].bitcast(I32).rearrange("p (e n) -> p e n", e=2)
        tok_f = probs[:, 0, 1, 2, 0:P]
        tok_bf = probs[:, 0, 1, 3, 0:P].bitcast(BF16).rearrange("p (e n) -> p e n", e=2)
        iota_i = probs[:, 0, 1, 4, :].bitcast(I32)
        code_bc = [probs[:, 1, 0, i, :].bitcast(BF16).rearrange("p (e n) -> p e n", e=2) for i in range(TURN)]
        halves = [stack[1][:, side, :, :].rearrange("p h s -> p (h s)").bitcast(BF16)
                  .rearrange("p (e n) -> p e n", e=2) for side in range(2)]
        code_part = [halves[0], halves[1], halves[0],
                     probs[:, 1, 0, 0:TURN, :].rearrange("p k n -> p (k n)").bitcast(BF16)
                     .rearrange("p (e n) -> p e n", e=2)]
        onehot = [probs[:, 1, 1, i, :].bitcast(BF16).rearrange("p (e n) -> p e n", e=2) for i in range(2)]

        m_bank = [bank(f"m_bank{i}") for i in range(2)]
        s_bank = [bank(f"s_bank{i}") for i in range(2)]
        o_bank = bank("o_bank")
        l_bank = bank("l_bank")
        a_bank = bank("a_bank")
        b_bank = bank("b_bank")
        shared = [a_bank, b_bank]

        tables_loaded = sem("tables_loaded")
        loaded = sem("loaded")
        tok_loaded = sem("tok_loaded")
        const = sem("const")
        vconst = sem("vconst")
        pconst = sem("pconst")
        codes_stored = sem("codes_stored")
        code_loaded = [sem(f"code_loaded{i}") for i in range(TURN)]
        part_loaded = [sem(f"part_loaded{i}") for i in range(len(CODE_PARTS))]
        onehot_done = sem("onehot_done")
        bias_copied = sem("bias_copied")
        emb_ready = sem("emb_ready")
        h_done = sem("h_done")
        x_ready = sem("x_ready")
        xt_ready = sem("xt_ready")
        xh_done = sem("xh_done")
        x_split = sem("x_split")
        qk_ready = sem("qk_ready")
        qk_hi = sem("qk_hi")
        qk_split = sem("qk_split")
        stacked = [sem(f"stacked{g}") for g in range(GROUPS)]
        v_ready = sem("v_ready")
        v_done = sem("v_done")
        m_ready = sem("m_ready")
        m_used = sem("m_used")
        nm_high = sem("nm_high")
        nm_split = sem("nm_split")
        nmt_ready = sem("nmt_ready")
        nm_row = sem("nm_row")
        nm_loaded = [sem(f"nm_loaded{g}") for g in range(GROUPS)]
        s_ready = sem("s_ready")
        exp_done = sem("exp_done")
        masked = sem("masked")
        tail_two = sem("tail_two")
        tail_three = sem("tail_three")
        tail_done = sem("tail_done")
        mix_done = sem("mix_done")
        sum_log = sem("sum_log")
        inv_ready = sem("inv_ready")
        mixed_done = sem("mixed_done")
        h_bo_ready = sem("h_bo_ready")
        y_ready = sem("y_ready")
        res_done = sem("res_done")
        bn2_done = sem("bn2_done")
        mv2_done = sem("mv2_done")
        log2_done = sem("log2_done")
        rstd2_done = sem("rstd2_done")
        shift2_done = sem("shift2_done")
        x2_ready = sem("x2_ready")
        ft_ready = sem("ft_ready")
        ft_done = sem("ft_done")
        fo_ready = sem("fo_ready")
        out_ready = sem("out_ready")
        out_stored = sem("out_stored")
        bn1_done = sem("bn1_done")
        mv1_done = sem("mv1_done")
        log1_done = sem("log1_done")
        rstd1_done = sem("rstd1_done")
        shift1_done = sem("shift1_done")

        held = {e: sem(f"held_{n}") for n, e in (("sp", mybir.EngineType.SP), ("pool", mybir.EngineType.Pool),
                                                 ("dve", mybir.EngineType.DVE))}

        class Row:

            def __init__(self, b, parity, looped):
                self.b, self.parity, self.looped = b, parity, looped

            def has(self, d):
                return self.looped or 0 <= self.b + d < BATCH

            def par(self, d):
                return (self.parity + d) % 2

        def is_row(n, number):
            return isinstance(n, int) and n == number

        def await_count(eng, semaphore, value):
            if not isinstance(value, int) or value > 0:
                eng.wait_ge(semaphore, value)

        def hold(eng):
            eng.sem_inc(held[eng.engine], 1)

        def over_rows(eng, iteration):
            for b in range(4):
                iteration(Row(b, b % 2, False))
            with eng.Fori(2, BATCH // 2 - 1) as pair:
                iteration(Row(2 * pair, 0, True))
                iteration(Row(2 * pair + 1, 1, True))
            for b in range(BATCH - 2, BATCH + 2):
                iteration(Row(b, b % 2, False))

        FILL = [Row(-2, 0, False), Row(-1, 1, False)]

        def embed_turns(eng, row, r, turn_of):
            if row is FILL[1] and r in EMBED_AT:
                with eng.Fori(*EMBED_AT[r]) as turn:
                    for i in range(TURN):
                        turn_of(turn, i, r)

        def row_done(n):
            return n + 1 if isinstance(n, int) else BATCH

        def weight_bank(row, r):
            return (-1, r + STEPS - LAG) if r < LAG else (0, r - LAG)

        def jobs_at(jobs, at):
            return [(-int(step // STEPS), name, c) for step, name, c in jobs if step % STEPS == at]

        READERS = {("x", 0): (x_split, 1, 1), **{("qk", c): (qk_split, 4, c + 1) for c in range(4)},
                   ("v", 0): (v_done, 2, 1), ("v", 1): (v_done, 2, 2), ("max", 0): (nm_row, 2, 1),
                   ("max", 1): (nm_row, 2, 2), ("y", 0): (res_done, 1, 1), ("ft", 0): (ft_done, 1, 1),
                   ("fo", 0): (out_ready, 1, 1)}
        BANK_JOBS = sorted(((step % STEPS, -int(step // STEPS), (name, c))
                              for step, name, c in PE_JOBS if (name, c) in READERS), key=lambda entry: entry[0])
        assert len(BANK_JOBS) % 2 == 0

        def place_of(job):
            return [entry[2] for entry in BANK_JOBS].index(job)

        def bank_of(name, c=0):
            return shared[place_of((name, c)) % 2]

        def await_bank(eng, row, name, c=0):
            for back in range(2, 3 * len(BANK_JOBS), 2):
                k = place_of((name, c)) - back
                d = BANK_JOBS[k % len(BANK_JOBS)][1] + k // len(BANK_JOBS)
                if row.has(d):
                    semaphore, per_row, n = READERS[BANK_JOBS[k % len(BANK_JOBS)][2]]
                    await_count(eng, semaphore, per_row * (row.b + d) + n)
                    return

        LAST = BATCH - 1

        def add_tails(eng, n, pair):
            g, half = divmod(pair, 2)
            banks = probs[:, g, half, :, :]
            sums = tail[g][:, 2 * half:2 * half + 2, :]
            eng.wait_ge(masked, 4 * n + pair + 1)
            eng.tensor_tensor(sums, banks[:, 0:3:2, P:4 * P], banks[:, 1:4:2, 0:3 * P],
                              ALU.add).then_inc(tail_two, 1)
            eng.wait_ge(tail_two, 4 * n + pair + 1)
            eng.tensor_tensor(sums[:, :, P:3 * P], sums[:, :, P:3 * P],
                              banks[:, 4, :].rearrange("p (h s) -> p h s", h=2), ALU.add).then_inc(tail_three, 1)
            eng.wait_ge(tail_three, 4 * n + pair + 1)
            eng.tensor_tensor(sums[:, :, 2 * P:3 * P], sums[:, :, 2 * P:3 * P], banks[:, 1:4:2, 3 * P:4 * P],
                              ALU.add).then_inc(tail_done, 1)

        block = ctx.enter_context(nc.Block())

        @block.sync
        def _(sp):
            sp.dma_start(tok, x.rearrange("b (q n) -> (b q) n", n=P)).then_inc(tok_loaded, 16)
            sp.dma_start(emb_in[:, 0:C], emb1).then_inc(tables_loaded, 16)
            sp.dma_start(emb_in[:, C:2 * C], emb2).then_inc(tables_loaded, 16)
            sp.dma_start(tokw_in[0:C, :], tok_w).then_inc(tables_loaded, 16)
            with nc.allow_non_contiguous_dma("weights and broadcasts, once"):
                sp.dma_start(tok_b_bc[:], tok_b.partition_broadcast(P)).then_inc(tables_loaded, 16)
                sp.wait_ge(vconst, 6)
                sp.dma_start(codes_dram.rearrange("e (p n) -> p e n", n=P), tok_bf).then_inc(codes_stored, 16)
                sp.wait_ge(codes_stored, 16)

            for i in range(TURN):
                sp.dma_start(code_bc[i], codes_dram[:, i * SEQ:(i + 1) * SEQ].partition_broadcast(P)
                             ).then_inc(code_loaded[i], 16)
            with nc.allow_non_contiguous_dma("weights and broadcasts, once"):
                for half in (0, C):
                    for n, w in enumerate((wq, wk, wv)):
                        sp.dma_start(stage[half:half + C, n * H * D:(n + 1) * H * D], w).then_inc(loaded, 16)
                sp.dma_start(ffnw_in[0:C, :], ffn_w).then_inc(loaded, 16)
                sp.dma_start(wo_sb[:], wo.rearrange("(g p) c -> p g c", p=P)).then_inc(loaded, 16)
                sp.dma_start(ffn_b_col[C:P, :], ffn_b.unsqueeze(1)).then_inc(loaded, 16)
                sp.dma_start(bo_bc[:], bo.partition_broadcast(P)).then_inc(loaded, 16)
            for part, (first, last) in enumerate(CODE_PARTS):
                if part == 2:
                    sp.wait_ge(onehot_done, TURN * CODE_PARTS[0][1])
                if part == 3:
                    sp.wait_ge(onehot_done, TURN)
                sp.dma_start(code_part[part][:, :, 0:(last - first) * TURN * SEQ],
                             codes_dram[:, first * TURN * SEQ:last * TURN * SEQ].partition_broadcast(P)
                             ).then_inc(part_loaded[part], 16)

            def load_max_rows(row, d, g):
                if row.has(d):
                    n = row.b + d
                    sp.wait_ge(nm_row, 2 * n + g + 1)
                    sp.dma_start(stack[row.par(d)][ALIBI_ROWS:ALL_ROWS, 0, g * HG:(g + 1) * HG, :].bitcast(F32),
                                 nm_rows[g][:].bitcast(F32)).then_inc(nm_loaded[g], 16)

            def load_stacks(row, g):
                if row.has(1):
                    n = row.b + 1
                    await_count(sp, s_ready, STEPS * (n - 2) + UNIT_BANKS * (g + 1))
                    hold(sp)
                    sp.wait_ge(qk_split, 4 * n + 2 * g + 2)
                    for j in range(HG):
                        for s, parts in enumerate((slice(0, 3, 2), slice(1, 3), slice(1, 4, 2))):
                            sp.dma_start(stack[row.par(1)][s * D:(s + 1) * D, :, g * HG + j, :].bitcast(F32),
                                         nat[g][j * D:(j + 1) * D, parts, :].bitcast(F32)).then_inc(stacked[g], 16)

            def iteration(row):
                load_max_rows(row, -1, 1)
                load_stacks(row, 0)
                load_max_rows(row, 0, 0)
                load_stacks(row, 1)
                if row.has(-2):
                    n = row.b - 2
                    sp.wait_ge(out_ready, n + 1)
                    sp.dma_start(out_rows[n] if isinstance(n, int) else
                                 out_rows[bass.ds(n, 1)].rearrange("o p t c -> (o p) t c"),
                                 out_sb[:]).then_inc(out_stored, 16)

            for row in FILL:
                iteration(row)
            sp.wait_ge(onehot_done, BATCH)
            sp.wait_ge(const, BIAS_STEPS)
            sp.dma_start(stack[1][QK_ROWS:ALL_ROWS, :, :, :].bitcast(F32),
                         stack[0][QK_ROWS:ALL_ROWS, :, :, :].bitcast(F32)).then_inc(bias_copied, 16)
            over_rows(sp, iteration)
            sp.wait_ge(out_stored, 16 * BATCH)

        @block.gpsimd
        def _(pool):
            count = [0]

            def step(ins):
                count[0] += 1
                ins.then_inc(const, 1)
                pool.wait_ge(const, count[0])

            step(pool.memset(ident[:], 0.0))
            step(pool.affine_select(out=ident[:], in_=ident[:], compare_op=ALU.not_equal, fill=1.0, base=0,
                                    pattern=[[-1, P]], channel_multiplier=1))
            step(pool.iota(code_id[:], pattern=[[0, 1]], base=0, channel_multiplier=1,
                           allow_small_or_imprecise_dtypes=True))
            step(pool.memset(eps[:], EPS))
            step(pool.memset(causal[:], 0.0))
            step(pool.affine_select(out=causal[:, SEQ - P:SEQ], in_=causal[:, SEQ - P:SEQ], compare_op=ALU.is_ge, fill=MASKED, base=0,
                                    pattern=[[-1, P]], channel_multiplier=1))
            step(pool.memset(ones[:], 1.0))
            assert count[0] == CONST_STEPS

            def diagonals(row, d, pair):
                if row.has(d):
                    n = row.b + d
                    g, half = divmod(pair, 2)
                    pool.wait_ge(exp_done, STEPS * n + PAIR_BANKS * (pair + 1))
                    hold(pool)
                    banks = probs[:, g, half, :, :]
                    for part, width in ((banks[:, :, 0:P], 5), (banks[:, 1:4:2, 3 * P:4 * P], 2),
                                        (banks[:, 4:5, 2 * P:3 * P], 1)):
                        ins = pool.affine_select(out=part, in_=part, compare_op=ALU.is_ge, fill=0.0, base=0,
                                                 pattern=[[0, width], [1, P]], channel_multiplier=-1)
                    ins.then_inc(masked, 1)
                    if not is_row(n, LAST):
                        add_tails(pool, n, pair)

            def add_out_bias(row, d, _):
                if row.has(d):
                    n = row.b + d
                    await_count(pool, res_done, n)
                    pool.wait_ge(h_done, row_done(n))
                    pool.tensor_tensor(h_bo[:], h_all[:, n, :, :] if isinstance(n, int) else
                                       h_all[:, bass.ds(n, 1), :, :].rearrange("p o t c -> p (o t) c"),
                                       bo_bc[:, :].unsqueeze(1).broadcast_to([P, T, C]),
                                       ALU.add).then_inc(h_bo_ready, 1)

            work = {"diagonals": diagonals, "h_bo": add_out_bias}

            def iteration(row):
                for r in range(STEPS):
                    for d, name, c in jobs_at(POOL_JOBS, r):
                        work[name](row, d, c)

            iteration(FILL[0])
            step(pool.iota(iota_i, pattern=[[1, SEQ]], base=0, channel_multiplier=0))
            step(pool.tensor_copy(pos, iota_i))
            for n, (value, row_value, at) in enumerate(
                    [(0.0, None, 1), (0.0, 1.0, 0), (0.0, None, 0), (1.0, 0.0, 0)]):
                step(pool.memset(coef[:, n, :], value))
                if row_value is None:
                    for h in range(H):
                        step(pool.affine_select(out=coef[:, n, h:h + 1], in_=coef[:, n, h:h + 1],
                                                compare_op=ALU.not_equal,
                                                fill=-SLOPES[h] if at else SLOPES[h], base=-(QK_ROWS + at),
                                                pattern=[[0, 1]], channel_multiplier=1))
                else:
                    step(pool.affine_select(out=coef[:, n, :], in_=coef[:, n, :], compare_op=ALU.not_equal,
                                            fill=row_value, base=-(QK_ROWS + at), pattern=[[0, H]],
                                            channel_multiplier=1))
            for side in range(2):
                for h in range(H):
                    step(pool.tensor_scalar(stack[0][QK_ROWS:ALL_ROWS, side, h, :], pos[QK_ROWS:ALL_ROWS, :],
                                            coef[QK_ROWS:ALL_ROWS, 2 * side, h:h + 1],
                                            coef[QK_ROWS:ALL_ROWS, 2 * side + 1, h:h + 1], ALU.mult, ALU.add))
            assert count[0] == BIAS_STEPS
            iteration(FILL[1])
            over_rows(pool, iteration)

        @block.scalar
        def _(act):
            def tanh_row(turn, i, _=0):
                b = TURN * turn + i
                act.wait_ge(emb_ready, b + 1)
                dst = (h_all[:, b, :, :].rearrange("p t c -> p (t c)") if isinstance(b, int) else
                       h_all[:, bass.ds(b, 1), :, :].rearrange("p o t c -> p (o t c)"))
                act.activation(dst, m_bank[i % 2][:, 0:T * C], ACT.Tanh).then_inc(h_done, 1)

            act.preload_act_table_set("exp_and_others")
            act.wait_ge(const, CONST_STEPS)
            for i in range(TURN):
                tanh_row(0, i)

            def exp_bank(row, r):
                d, idx = weight_bank(row, r)
                if not row.has(d):
                    return
                n, g = row.b + d, idx // UNIT_BANKS
                half, k = divmod(idx % UNIT_BANKS, PAIR_BANKS)
                if idx % UNIT_BANKS == 0:
                    await_count(act, mix_done, 8 * (n - 1) + 4 * g + 4)
                act.wait_ge(s_ready, STEPS * n + idx + 1)
                act.activation(probs[:, g, half, k, :], s_bank[idx % 2][:], ACT.Exp).then_inc(exp_done, 1)

            def x_high(row, d, _):
                if row.has(d):
                    n = row.b + d
                    act.wait_ge(xt_ready, n + 1)
                    await_count(act, v_ready, 2 * (n - 2) + 2)
                    act.copy(xs[row.par(d)][:], bank_of("x")[:]).then_inc(xh_done, 1)

            def qk_high(row, d, c):
                if row.has(d):
                    n, g = row.b + d, c // 2
                    await_count(act, stacked[g], 16 * STACK_DMAS * n)
                    act.wait_ge(qk_ready, 4 * n + c + 1)
                    if c % 2 == 0:
                        ins = act.mul(nat[g][:, 1, :], bank_of("qk", c)[:], SCALE)
                    else:
                        ins = act.copy(nat[g][:, 2, :], bank_of("qk", c)[:])
                    ins.then_inc(qk_hi, 1)

            def copy_values(row, d, c):
                if row.has(d):
                    n = row.b + d
                    await_count(act, mix_done, 8 * (n - 2) + 8)
                    act.wait_ge(v_ready, 2 * n + c + 1)
                    act.copy(values[row.par(d)][:, 2 * c:2 * c + 2, :, :],
                             bank_of("v", c)[:].rearrange("p (t h d) -> p t h d", t=2, h=H)).then_inc(v_done, 1)

            def copy_max_rows(row, d, g):
                if row.has(d):
                    n = row.b + d
                    await_count(act, nm_loaded[g], 16 * n)
                    act.wait_ge(nmt_ready, 2 * n + g + 1)
                    act.copy(nm_rows[g][:], bank_of("max", g)[0:2 * HG * T, 0:P]).then_inc(nm_row, 1)

            def log_sums(row, d, g):
                if row.has(d):
                    n = row.b + d
                    act.wait_ge(mix_done, 8 * n + 4 * g + 4)
                    act.activation(log_sum[:], l_bank[:], ACT.Ln).then_inc(sum_log, 1)

            def invert_sums(row, d, g):
                if row.has(d):
                    n = row.b + d
                    await_count(act, mixed_done, 2 * n + g)
                    act.wait_ge(sum_log, 2 * n + g + 1)
                    act.activation(inv_sum[:], log_sum[:], ACT.Exp, scale=-1.0).then_inc(inv_ready, 1)

            def rsqrt(n, which, mv, mv_done, log_done, rstd, rstd_used, rstd_done):
                act.wait_ge(mv_done, n + 1)
                act.activation(logv[:, which, :].unsqueeze(2), mv[:, :, 1:2], ACT.Ln,
                               bias=eps[:, 0:1]).then_inc(log_done, 1)
                await_count(act, rstd_used, n)
                act.wait_ge(log_done, n + 1)
                act.activation(rstd[:], logv[:, which, :], ACT.Exp, scale=-0.5).then_inc(rstd_done, 1)

            def rsqrt_first(row, d, _):
                if row.has(d):
                    rsqrt(row.b + d, 0, mv1, mv1_done, log1_done, rstd1, shift1_done, rstd1_done)

            def rsqrt_second(row, d, _):
                if row.has(d):
                    rsqrt(row.b + d, 1, mv2, mv2_done, log2_done, rstd2, shift2_done, rstd2_done)

            def first_layernorm(row, d, c):
                if row.has(d):
                    n = row.b + d
                    act.wait_ge(shift1_done, n + 1)
                    await_count(act, xt_ready, n)
                    for t in (2 * c, 2 * c + 1):
                        h = (h_all[:, n, t, :] if isinstance(n, int) else
                             h_all[:, bass.ds(n, 1), t, :].rearrange("p o c -> p (o c)"))
                        ins = act.activation(x2[:, t, :, :], h.unsqueeze(1).broadcast_to([P, 2, C]), ACT.Identity,
                                             bias=shift1[:, t:t + 1], scale=rstd1[:, t:t + 1])
                    ins.then_inc(x_ready, 1)

            def second_layernorm(row, d, c):
                if row.has(d):
                    n = row.b + d
                    act.wait_ge(shift2_done, n + 1)
                    await_count(act, ft_ready, n)
                    for t in (2 * c, 2 * c + 1):
                        ins = act.activation(ffn_in[:, t, 0, :], ffn_in[:, t, 1, :], ACT.Identity,
                                             bias=shift2[:, t:t + 1], scale=rstd2[:, t:t + 1])
                    ins.then_inc(x2_ready, 1)

            def copy_ffn_in(row, d, _):
                if row.has(d):
                    n = row.b + d
                    await_count(act, fo_ready, n)
                    act.wait_ge(ft_ready, n + 1)
                    act.activation(ffn_in_t[:], bank_of("ft")[:], ACT.Identity, bias=ffn_b_col[:, 0:1]).then_inc(ft_done, 1)

            def copy_out(row, d, _):
                if row.has(d):
                    n = row.b + d
                    await_count(act, out_stored, 16 * n)
                    act.wait_ge(fo_ready, n + 1)
                    act.copy(out_sb[:], bank_of("fo")[:, 0:T * C].rearrange("p (t c) -> p t c", t=T)).then_inc(out_ready, 1)

            work = {"rsqrt1": rsqrt_first, "x": x_high, "qk": qk_high, "v": copy_values, "max": copy_max_rows,
                    "log": log_sums, "norm": invert_sums, "rsqrt2": rsqrt_second, "apply1": first_layernorm, "apply2": second_layernorm, "ft": copy_ffn_in, "fo": copy_out}

            def iteration(row):
                for r in range(STEPS):
                    embed_turns(act, row, r, tanh_row)
                    if row is FILL[1] and r == max(EMBED_AT):
                        act.preload_act_table_set("natural_log_exp_and_others")
                    for d, name, c in jobs_at(ACT_JOBS, r):
                        work[name](row, d, c)
                    exp_bank(row, r)
                    for d, name, c in jobs_at(ACT_JOBS, r + 0.5):
                        work[name](row, d, c)

            act.preload_act_table_set("natural_log_exp_and_others")
            iteration(FILL[0])
            act.preload_act_table_set("exp_and_others")
            iteration(FILL[1])
            over_rows(act, iteration)

        @block.vector
        def _(dve):
            count = [0]

            def step(ins):
                count[0] += 1
                ins.then_inc(vconst, 1)
                dve.wait_ge(vconst, count[0])

            dve.wait_ge(tok_loaded, 16)
            step(dve.tensor_scalar(tok_code[:, 0, :], tok, SHIFT, None, ALU.arith_shift_right))
            step(dve.tensor_scalar(tok_code[:, 1, :], tok, CODES - 1, None, ALU.bitwise_and))
            step(dve.tensor_copy(tok_f, tok_code[:, 0, :]))
            step(dve.tensor_scalar(tok_f, tok_f, 0.0, float(CODES - 1), ALU.max, ALU.min))
            step(dve.tensor_copy(tok_bf[:, 0, :], tok_f))
            step(dve.tensor_copy(tok_bf[:, 1, :], tok_code[:, 1, :]))

            dve.wait_ge(tables_loaded, 16 * TABLE_LOADS)
            dve.wait_ge(pconst, 1)
            dve.tensor_copy(embT, a_bank[:, 0:P]).then_inc(vconst, 1)
            dve.tensor_copy(tokwT, a_bank[:, P:P + C]).then_inc(vconst, 1)
            count[0] += 2
            dve.wait_ge(pconst, 3)
            step(dve.tensor_tensor(tab_rest[:, 0, 0, :], b_bank[:, 0:C], tok_b_bc[:], ALU.add))
            step(dve.tensor_copy(tab_rest[:, 1, 0, :], o_bank[:, 0:C]))
            step(dve.tensor_copy(tabs[:, :, 0, :], tab_rest[:, :, 0, :]))
            step(dve.tensor_tensor(tab_rest[:, :, 1, :], tab_rest[:, :, 0, :], tabs[:, :, 0, :], ALU.subtract))
            step(dve.tensor_copy(tabs[:, :, 1, :], tab_rest[:, :, 1, :]))
            step(dve.tensor_tensor(tab_rest[:, :, 0, :], tab_rest[:, :, 1, :], tabs[:, :, 1, :], ALU.subtract))
            step(dve.tensor_copy(tabs[:, :, 2, :], tab_rest[:, :, 0, :]))
            assert count[0] == TABLE_STEPS

            dve.wait_ge(const, CONST_STEPS)

            def one_hot(turn, i, r=None):
                b = TURN * turn + i
                if r is None:
                    codes = code_bc[i]
                    dve.wait_ge(code_loaded[i], 16)
                else:
                    part = [first <= EMBED_AT[r][0] < last for first, last in CODE_PARTS].index(True)
                    codes = code_part[part][:, :, bass.ds((b - TURN * CODE_PARTS[part][0]) * SEQ, SEQ)]
                    dve.wait_ge(part_loaded[part], 16)
                await_count(dve, emb_ready, b - 1)
                dve.tensor_scalar(onehot[i % 2], codes, code_id[:, 0:1], None,
                                  ALU.is_equal).then_inc(onehot_done, 1)

            for i in range(TURN):
                one_hot(0, i)

            def maxima(row, r):
                if not row.has(0):
                    return
                g, idx = divmod(r, UNIT_BANKS)
                half, k = divmod(idx, PAIR_BANKS)
                src = m_bank[r % 2]
                dve.wait_ge(m_ready, STEPS * row.b + r + 1)
                hold(dve)
                for hh, extent, col in bank_blocks(k):
                    ins = dve.tensor_tensor_reduce(out=unused[:, r % 2, col:col + extent * P],
                                                   in0=src[:, col:col + extent * P], in1=causal[:, SEQ - extent * P:SEQ],
                                                   scale=1.0, scalar=MASKED, op0=ALU.add, op1=ALU.max,
                                                   accum_out=row_max[g][:, 2 * half + hh, extent - 1:extent])
                ins.then_inc(m_used, 1)

            def split_max(row, d, g):
                if row.has(d):
                    n = row.b + d
                    await_count(dve, nmt_ready, 2 * (n - 1) + g + 1)
                    dve.wait_ge(m_used, STEPS * n + UNIT_BANKS * (g + 1))
                    dve.tensor_scalar(nm_parts[g][:, 0, :, :], row_max[g][:], -1.0, None,
                                      ALU.mult).then_inc(nm_high, 1)
                    dve.wait_ge(nm_high, 2 * n + g + 1)
                    dve.scalar_tensor_tensor(out=nm_parts[g][:, 1, :, :], in0=row_max[g][:], scalar=-1.0,
                                             in1=nm_parts[g][:, 0, :, :].bitcast(F32), op0=ALU.mult,
                                             op1=ALU.subtract).then_inc(nm_split, 1)

            def x_low(row, d, _):
                if row.has(d):
                    n = row.b + d
                    lo = xs[row.par(d)][C:P, :]
                    dve.wait_ge(xh_done, n + 1)
                    dve.tensor_tensor(lo, bank_of("x")[C:P, :], lo.bitcast(F32), ALU.subtract).then_inc(x_split, 1)

            def qk_low(row, d, c):
                if row.has(d):
                    n, g = row.b + d, c // 2
                    dve.wait_ge(qk_hi, 4 * n + c + 1)
                    if c % 2 == 0:
                        ins = dve.scalar_tensor_tensor(out=nat[g][:, 0, :], in0=bank_of("qk", c)[:], scalar=SCALE,
                                                       in1=nat[g][:, 1, :].bitcast(F32), op0=ALU.mult,
                                                       op1=ALU.subtract)
                    else:
                        ins = dve.tensor_tensor(nat[g][:, 3, :], bank_of("qk", c)[:], nat[g][:, 2, :].bitcast(F32),
                                                ALU.subtract)
                    ins.then_inc(qk_split, 1)

            def normalise(row, d, g):
                if row.has(d):
                    n = row.b + d
                    await_count(dve, y_ready, n)
                    dve.wait_ge(inv_ready, 2 * n + g + 1)
                    dve.tensor_tensor(mixed[g][:], o_bank[:], inv_sum[:], ALU.mult).then_inc(mixed_done, 1)

            def residual(row, d, _):
                if row.has(d):
                    n = row.b + d
                    dve.wait_ge(h_bo_ready, n + 1)
                    await_count(dve, ft_ready, n)
                    dve.wait_ge(y_ready, n + 1)
                    dve.tensor_tensor(ffn_in[:, :, 1, :], bank_of("y")[:, 0:T * C].rearrange("p (t c) -> p t c", t=T),
                                      h_bo[:], ALU.add).then_inc(res_done, 1)

            def second_statistics(row, d, _):
                if row.has(d):
                    n = row.b + d
                    dve.wait_ge(res_done, n + 1)
                    for t in range(T):
                        ins = dve.bn_stats(bn2[:, t, :], ffn_in[:, t, 1, :])
                    ins.then_inc(bn2_done, 1)

            def second_moments(row, d, _):
                if row.has(d):
                    n = row.b + d
                    dve.wait_ge(bn2_done, n + 1)
                    await_count(dve, rstd2_done, n)
                    hold(dve)
                    for t in range(T):
                        ins = dve.bn_aggr(mv2[:, t, :], bn2[:, t, :])
                    ins.then_inc(mv2_done, 1)

            def first_statistics(row, d, _):
                if row.has(d):
                    n = row.b + d
                    for t in range(T):
                        src = (h_all[:, n, t, :] if isinstance(n, int) else
                               h_all[:, bass.ds(n, 1), t, :].rearrange("p o c -> p (o c)"))
                        if t == 0:
                            dve.wait_ge(h_done, row_done(n))
                        ins = dve.bn_stats(bn1[:, t, :], src)
                    ins.then_inc(bn1_done, 1)

            def first_moments(row, d, _):
                if row.has(d):
                    n = row.b + d
                    dve.wait_ge(bn1_done, n + 1)
                    await_count(dve, rstd1_done, n)
                    hold(dve)
                    for t in range(T):
                        ins = dve.bn_aggr(mv1[:, t, :], bn1[:, t, :])
                    ins.then_inc(mv1_done, 1)

            def shift(n, mv, rstd, rstd_done, before_used, to, done):
                await_count(dve, before_used, 2 * n)
                dve.wait_ge(rstd_done, n + 1)
                dve.scalar_tensor_tensor(out=to[:, :].unsqueeze(2), in0=mv[:, :, 0:1], scalar=-1.0,
                                         in1=rstd[:, :].unsqueeze(2), op0=ALU.mult, op1=ALU.mult).then_inc(done, 1)

            def shift_first(row, d, _):
                if row.has(d):
                    shift(row.b + d, mv1, rstd1, rstd1_done, x_ready, shift1, shift1_done)

            def shift_second(row, d, _):
                if row.has(d):
                    shift(row.b + d, mv2, rstd2, rstd2_done, x2_ready, shift2, shift2_done)

            def last_tails(row, d, pair):
                if is_row(row.b, LAST - d):
                    add_tails(dve, LAST, pair)

            work = {"tails": last_tails, "shift1": shift_first, "shift2": shift_second, "bn1": first_statistics, "moments1": first_moments, "x": x_low, "qk": qk_low, "max": split_max, "norm": normalise,
                    "y": residual, "bn2": second_statistics, "moments2": second_moments}

            def iteration(row):
                for r in range(STEPS):
                    embed_turns(dve, row, r, one_hot)
                    for d, name, c in jobs_at(DVE_JOBS, r):
                        work[name](row, d, c)
                    maxima(row, r)
                    for d, name, c in jobs_at(DVE_JOBS, r + 0.5):
                        work[name](row, d, c)

            iteration(FILL[0])
            dve.wait_ge(loaded, 16 * LOADS)
            step(dve.tensor_copy(w_hi[:], stage))
            step(dve.tensor_tensor(w_lo[:], stage, w_hi[:].bitcast(F32), ALU.subtract))
            step(dve.tensor_copy(ffn_rhs[C:P, :], ident[C:P, C:P]))
            dve.wait_ge(pconst, 4)
            step(dve.tensor_copy(ffn_rhs[0:C, :], a_bank[0:C, 2 * P:2 * P + C]))
            step(dve.memset(ffn_b_col[0:C, :], 0.0))
            assert count[0] == SETUP_STEPS
            iteration(FILL[1])
            over_rows(dve, iteration)

        @block.tensor
        def _(pe):
            pe.wait_ge(const, CONST_STEPS)
            pe.wait_ge(tables_loaded, 16 * TABLE_LOADS)
            pe.transpose(a_bank[:, 0:P], emb_in, ident[:])
            pe.transpose(a_bank[:, P:P + C], tokw_in[0:C, :], ident[0:C, 0:C]).then_inc(pconst, 1)
            pe.wait_ge(vconst, 8)
            pe.matmul(b_bank[:, 0:C], embT[0:C, :], tokwT[0:C, :], start=True, stop=True).then_inc(pconst, 1)
            pe.matmul(o_bank[:, 0:C], embT[C:P, :], tokwT[C:P, :], start=True, stop=True).then_inc(pconst, 1)
            pe.wait_ge(vconst, TABLE_STEPS)

            def embed(turn, i, _=0):
                b = TURN * turn + i
                pe.wait_ge(onehot_done, b + 1)
                await_count(pe, h_done, b - 1)
                for t in range(T):
                    for e in range(2):
                        for part in range(3):
                            ins = pe.matmul(m_bank[i % 2][:, t * C:(t + 1) * C],
                                            onehot[i % 2][:, e, t * P:(t + 1) * P], tabs[:, e, part, :],
                                            start=(e == 0 and part == 0), stop=(e == 1 and part == 2))
                ins.then_inc(emb_ready, 1)

            for i in range(TURN):
                embed(0, i)
            def max_scores(row, r):
                if not row.has(0):
                    return
                g, idx = divmod(r, UNIT_BANKS)
                half, k = divmod(idx, PAIR_BANKS)
                st, dst = stack[row.par(0)], m_bank[r % 2]
                if idx == 0:
                    pe.wait_ge(stacked[g], 16 * STACK_DMAS * (row.b + 1))
                await_count(pe, m_used, STEPS * row.b + r - 1)
                for hh, extent, col in bank_blocks(k):
                    head, diag = g * HG + 2 * half + hh, (extent - 1) * P
                    ins = pe.matmul(dst[:, col:col + extent * P], st[0:ALIBI_ROWS, 0, head, diag:diag + P],
                                    st[0:ALIBI_ROWS, 1, head, 0:extent * P], start=True, stop=True)
                ins.then_inc(m_ready, 1)

            def weight_scores(row, r):
                d, index = weight_bank(row, r)
                if not row.has(d):
                    return
                n = row.b + d
                g, idx = divmod(index, UNIT_BANKS)
                half, k = divmod(idx, PAIR_BANKS)
                st, dst = stack[row.par(d)], s_bank[index % 2]
                if idx == 0:
                    pe.wait_ge(nm_loaded[g], 16 * (n + 1))
                await_count(pe, exp_done, STEPS * n + index - 1)
                for hh, extent, col in bank_blocks(k):
                    head, first = g * HG + 2 * half + hh, SEQ - extent * P
                    ins = pe.matmul(dst[:, col:col + extent * P], st[0:ALL_ROWS, 1, head, first:first + P],
                                    st[0:ALL_ROWS, 0, head, first:SEQ], start=True, stop=True)
                ins.then_inc(s_ready, 1)

            def mix(row, d, c):
                if not row.has(d):
                    return
                n = row.b + d
                g, i = divmod(c, T)
                if i == 0:
                    pe.wait_ge(masked, 4 * n + 2 * g + 2)
                    pe.wait_ge(v_done, 2 * n + 2)
                    await_count(pe, sum_log, 2 * n + g)
                    await_count(pe, mixed_done, 2 * n + g)
                for hh in range(HG):
                    k, col = block_place(hh % 2, T - i)
                    ins = pe.matmul(o_bank[hh * D:(hh + 1) * D, i * P:SEQ], values[row.par(d)][:, i, g * HG + hh, :],
                                    probs[:, g, hh // 2, k, col:col + SEQ - i * P],
                                    start=(i == 0), stop=(i == T - 1))
                if i == T - 1:
                    pe.wait_ge(tail_done, 4 * n + 2 * g + 2)
                for hh in range(HG):
                    k, col = block_place(hh % 2, T - i)
                    if i == 0:
                        first, last, weights = 0, P, probs[:, g, hh // 2, k, col:col + P]
                    elif i == T - 1:
                        first, last, weights = P, SEQ, tail[g][:, hh, :]
                    else:
                        continue
                    ins = pe.matmul(l_bank[hh * D:(hh + 1) * D, first:last], ones[:], weights,
                                    start=True, stop=True, skip_group_check=True)
                ins.then_inc(mix_done, 1)

            def transpose_x(row, d, _):
                if row.has(d):
                    n = row.b + d
                    await_bank(pe, row, "x")
                    pe.wait_ge(x_ready, 2 * n + 2)
                    for t in range(T):
                        ins = pe.transpose(bank_of("x")[:, t * P:(t + 1) * P],
                                           x2[:, t, :, :].rearrange("p a c -> p (a c)"), ident[:])
                    ins.then_inc(xt_ready, 1)

            def project_qk(row, d, c):
                if row.has(d):
                    n, g = row.b + d, c // 2
                    cols = slice((c % 2) * H * D + g * P, (c % 2) * H * D + (g + 1) * P)
                    await_bank(pe, row, "qk", c)
                    if c == 0:
                        pe.wait_ge(x_split, n + 1)
                    pe.matmul(bank_of("qk", c)[:], w_hi[:, cols], xs[row.par(d)][:], start=True, stop=False)
                    pe.matmul(bank_of("qk", c)[:], w_lo[:, cols], xs[row.par(d)][:], start=False,
                              stop=True).then_inc(qk_ready, 1)

            def project_v(row, d, c):
                if row.has(d):
                    n = row.b + d
                    await_bank(pe, row, "v", c)
                    for tt in range(2):
                        t = 2 * c + tt
                        for w in (w_hi, w_lo):
                            ins = pe.matmul(bank_of("v", c)[:, tt * H * D:(tt + 1) * H * D],
                                            xs[row.par(d)][:, t * P:(t + 1) * P], w[:, 2 * H * D:3 * H * D],
                                            start=(w is w_hi), stop=(w is w_lo))
                    ins.then_inc(v_ready, 1)

            def transpose_max(row, d, g):
                if row.has(d):
                    n = row.b + d
                    await_bank(pe, row, "max", g)
                    pe.wait_ge(nm_split, 2 * n + g + 1)
                    pe.transpose(bank_of("max", g)[0:2 * HG * T, 0:P],
                                 nm_parts[g][:].bitcast(F32).rearrange("p a h t -> p (a h t)"),
                                 ident[:]).then_inc(nmt_ready, 1)

            def project_out(row, d, _):
                if row.has(d):
                    n = row.b + d
                    await_bank(pe, row, "y")
                    pe.wait_ge(mixed_done, 2 * n + 2)
                    for t in range(T):
                        for g in range(GROUPS):
                            ins = pe.matmul(bank_of("y")[:, t * C:(t + 1) * C], mixed[g][:, t * P:(t + 1) * P],
                                            wo_sb[:, g, :], start=(g == 0), stop=(g == GROUPS - 1))
                    ins.then_inc(y_ready, 1)

            def transpose_ffn_in(row, d, _):
                if row.has(d):
                    n = row.b + d
                    await_bank(pe, row, "ft")
                    pe.wait_ge(x2_ready, 2 * n + 2)
                    for t in range(T):
                        ins = pe.transpose(bank_of("ft")[:, t * P:(t + 1) * P],
                                           ffn_in[:, t, :, :].rearrange("p a c -> p (a c)"), ident[:])
                    ins.then_inc(ft_ready, 1)

            def feed_forward(row, d, _):
                if row.has(d):
                    await_bank(pe, row, "fo")
                    pe.wait_ge(ft_done, row.b + d + 1)
                    for t in range(T):
                        ins = pe.matmul(bank_of("fo")[:, t * C:(t + 1) * C], ffn_in_t[:, t * P:(t + 1) * P],
                                        ffn_rhs[:], start=True, stop=True)
                    ins.then_inc(fo_ready, 1)

            work = {"x": transpose_x, "qk": project_qk, "v": project_v, "max": transpose_max, "mix": mix,
                    "y": project_out, "ft": transpose_ffn_in, "fo": feed_forward}

            def iteration(row):
                for r in range(STEPS):
                    embed_turns(pe, row, r, embed)
                    max_scores(row, r)
                    weight_scores(row, r)
                    for d, name, c in jobs_at(PE_JOBS, r):
                        work[name](row, d, c)

            iteration(FILL[0])
            pe.wait_ge(loaded, 16 * LOADS)
            pe.transpose(a_bank[0:C, 2 * P:2 * P + C], ffnw_in[0:C, :], ident[0:C, 0:C]).then_inc(pconst, 1)
            pe.wait_ge(vconst, SETUP_STEPS)
            iteration(FILL[1])
            pe.wait_ge(h_done, BATCH)
            pe.wait_ge(const, BIAS_STEPS)
            pe.wait_ge(bias_copied, 16)
            over_rows(pe, iteration)


TABLE_LOADS = 4
LOADS = 6 + 4
CONST_STEPS = 7
BIAS_STEPS = CONST_STEPS + 2 + 4 + 2 * H + 2 + 2 * H
TABLE_STEPS = 6 + 2 + 7
SETUP_STEPS = TABLE_STEPS + 5

_INS = ["x", "L0_tok_emb1", "L0_tok_emb2", "L0_tok_W", "L0_tok_b", "L0_attn_Wq", "L0_attn_Wk", "L0_attn_Wv",
        "L0_attn_Wo", "L0_attn_bo", "L0_ffn_weight", "L0_ffn_bias"]


def kernel(**inputs):
    import numpy as _np
    import concourse.bacc as _bacc
    from concourse import mybir as _mybir
    from concourse.bass_utils import run_bass_kernel_spmd as _run

    nc = _bacc.Bacc("TRN2", target_bir_lowering=False, num_devices=1)
    arrays, args = {}, []
    for name in _INS:
        a = _np.ascontiguousarray(inputs[name])
        arrays[f"in_{name}_dram"] = a
        args.append(nc.dram_tensor(f"in_{name}_dram", a.shape, _mybir.dt.from_np(a.dtype),
                                   kind="ExternalInput").ap())
    args.append(nc.dram_tensor("out_0_dram", (BATCH, SEQ, C), _mybir.dt.float32, kind="ExternalOutput").ap())
    build(nc, *args)
    r = _run(nc, [arrays], core_ids=[0])
    return r.results[0]["out_0_dram"]
```
